# Optimizing a Trainium2 kernel written in Bass

```python
import numpy as np
import jax
import jax.numpy as jnp

def _softmax(x, axis=-1):
    return jax.nn.softmax(x, axis=axis)
def _gelu(x):
    return jax.nn.gelu(x, approximate=True)
def _silu(x):
    return jax.nn.silu(x)
def _sigmoid(x):
    return jax.nn.sigmoid(x)
def _layernorm(x, axis=-1, eps=1e-5):
    m = jnp.mean(x, axis=axis, keepdims=True)
    v = jnp.var(x, axis=axis, keepdims=True)
    return (x - m) / jnp.sqrt(v + eps)
def _scatter_add(tgt, idx, src, axis=0):
    return tgt.at[idx].add(src)
def _segment_sum(src, seg, n):
    return jax.ops.segment_sum(src, seg, n)

kernel_name = 'mk_conv_preact_d2_conv_nchw1024_ae31a1'

def setup_inputs(seed: int = 0):
    np.random.seed(seed)
    _w = jnp.asarray
    def _rec_inputs():
        import jax
        import jax.numpy as jnp
        _gk = jax.random.key(seed)
        x = 0.0003368 + 1 * jax.random.normal(jax.random.fold_in(_gk, 1), (128, 1024, 14, 14), jnp.float32)
        return x
    x = _rec_inputs()
    def _L0_conv_setup():
        import jax, jax.numpy as jnp
        import numpy as np
        from functools import partial
        N = 14
        MAX_ITER = 10
        ERR_TH = 0.0001

        def _gauss_dist(n):
            coords = jnp.stack(jnp.meshgrid(jnp.arange(n), jnp.arange(n), indexing='ij'), axis=0)
            coords = coords.reshape(2, -1)
            d2 = jnp.sum((coords[:, :, None] - coords[:, None, :]) ** 2, axis=0).astype(jnp.float32)
            ep2 = (0.15 * n) ** 2
            return jnp.exp(-d2 / (2.0 * ep2))
        key = jax.random.key(seed)
        feature = jax.random.normal(key, (128, 1024, N, N), dtype=jnp.float32)
        return {'feature': feature}
    _L0_conv_all = _L0_conv_setup()
    _L0_conv_in = {k: v for k, v in _L0_conv_all.items() if k in ()}
    del _L0_conv_all

    def _L1_conv_setup():
        import jax, jax.numpy as jnp
        import numpy as np
        CP = 1.0
        DP = 2
        EPS = 1e-05

        def kerv2d(x, w, stride, padding):
            y = jax.lax.conv_general_dilated(x, w, window_strides=(stride, stride), padding=[(padding, padding), (padding, padding)], dimension_numbers=('NCHW', 'OIHW', 'NCHW'))
            return (y + CP) ** DP

        def bn(x, g, b, m, v):
            inv = g / jnp.sqrt(v + EPS)
            return x * inv[None, :, None, None] + (b - m * inv)[None, :, None, None]
        key = jax.random.key(seed)
        ks = jax.random.split(key, 4)
        C_in, C_mid = (1024, 256)
        d = {'x': jax.random.normal(ks[0], (128, C_in, 14, 14), jnp.float32), 'w1': jax.random.normal(ks[1], (C_mid, C_in, 1, 1), jnp.float32) * 0.03, 'w2': jax.random.normal(ks[2], (C_mid, C_mid, 3, 3), jnp.float32) * 0.02, 'w3': jax.random.normal(ks[3], (C_in, C_mid, 1, 1), jnp.float32) * 0.03}
        for i, c in zip((1, 2, 3), (C_mid, C_mid, C_in)):
            d[f'g{i}'] = jnp.ones((c,), jnp.float32)
            d[f'b{i}'] = jnp.zeros((c,), jnp.float32)
            d[f'm{i}'] = jnp.zeros((c,), jnp.float32)
            d[f'v{i}'] = jnp.ones((c,), jnp.float32)
        return d
    _L1_conv_all = _L1_conv_setup()
    _L1_conv_in = {k: v for k, v in _L1_conv_all.items() if k in ('w1', 'w2', 'w3', 'g1', 'b1', 'm1', 'v1', 'g2', 'b2', 'm2', 'v2', 'g3', 'b3', 'm3', 'v3', )}
    del _L1_conv_all

    return {
        "x": x,
        "L1_conv_w1": _L1_conv_in["w1"],
        "L1_conv_w2": _L1_conv_in["w2"],
        "L1_conv_w3": _L1_conv_in["w3"],
        "L1_conv_g1": _L1_conv_in["g1"],
        "L1_conv_b1": _L1_conv_in["b1"],
        "L1_conv_m1": _L1_conv_in["m1"],
        "L1_conv_v1": _L1_conv_in["v1"],
        "L1_conv_g2": _L1_conv_in["g2"],
        "L1_conv_b2": _L1_conv_in["b2"],
        "L1_conv_m2": _L1_conv_in["m2"],
        "L1_conv_v2": _L1_conv_in["v2"],
        "L1_conv_g3": _L1_conv_in["g3"],
        "L1_conv_b3": _L1_conv_in["b3"],
        "L1_conv_m3": _L1_conv_in["m3"],
        "L1_conv_v3": _L1_conv_in["v3"],
    }

def reference(x, L1_conv_w1, L1_conv_w2, L1_conv_w3, L1_conv_g1, L1_conv_b1, L1_conv_m1, L1_conv_v1, L1_conv_g2, L1_conv_b2, L1_conv_m2, L1_conv_v2, L1_conv_g3, L1_conv_b3, L1_conv_m3, L1_conv_v3):
    import jax
    import jax.numpy as jnp
    def _L0_conv_ref(feature):
        import jax, jax.numpy as jnp
        import numpy as np
        from functools import partial
        N = 14
        MAX_ITER = 10
        ERR_TH = 0.0001

        def _gauss_dist(n):
            coords = jnp.stack(jnp.meshgrid(jnp.arange(n), jnp.arange(n), indexing='ij'), axis=0)
            coords = coords.reshape(2, -1)
            d2 = jnp.sum((coords[:, :, None] - coords[:, None, :]) ** 2, axis=0).astype(jnp.float32)
            ep2 = (0.15 * n) ** 2
            return jnp.exp(-d2 / (2.0 * ep2))
        B, K, n, _ = feature.shape
        S = n * n
        f = feature.reshape(B, K, S)
        sq = jnp.sum(f * f, axis=1)
        G = jnp.einsum('bks,bkt->bst', f, f)
        d2 = jnp.maximum(sq[:, :, None] + sq[:, None, :] - 2.0 * G, 0.0)
        norm = jnp.where(d2 > 0, jnp.sqrt(jnp.where(d2 > 0, d2, 1.0)), 0.0)
        dist = _gauss_dist(n)
        D_ = norm * dist
        D = D_ / jnp.sum(D_, axis=1).reshape(B, S, 1)
        M0 = jnp.ones((B, S, 1), dtype=feature.dtype) / S

        def step(carry, _):
            M, done = carry
            newM = jnp.matmul(D, M)
            err = jnp.mean(jnp.abs(newM - M))
            newM = jnp.where(done, M, newM)
            done = done | (err < ERR_TH)
            return ((newM, done), None)
        (M, _), _ = jax.lax.scan(step, (M0, jnp.array(False)), None, length=MAX_ITER)
        return M.reshape(B, 1, n, n) * feature

    def _L1_conv_ref(x, w1, w2, w3, g1, b1, m1, v1, g2, b2, m2, v2, g3, b3, m3, v3):
        import jax, jax.numpy as jnp
        import numpy as np
        CP = 1.0
        DP = 2
        EPS = 1e-05

        def kerv2d(x, w, stride, padding):
            y = jax.lax.conv_general_dilated(x, w, window_strides=(stride, stride), padding=[(padding, padding), (padding, padding)], dimension_numbers=('NCHW', 'OIHW', 'NCHW'))
            return (y + CP) ** DP

        def bn(x, g, b, m, v):
            inv = g / jnp.sqrt(v + EPS)
            return x * inv[None, :, None, None] + (b - m * inv)[None, :, None, None]
        identity = x
        h = bn(kerv2d(x, w1, 1, 0), g1, b1, m1, v1)
        h = bn(kerv2d(h, w2, 1, 1), g2, b2, m2, v2)
        h = bn(kerv2d(h, w3, 1, 0), g3, b3, m3, v3)
        return h + identity

    def _gn(v, G=32, eps=1e-5):
        B_, C_, H_, W_ = v.shape
        g = v.reshape(B_, G, C_ // G, H_, W_)
        m = jnp.mean(g, axis=(2, 3, 4), keepdims=True)
        s = jnp.var(g, axis=(2, 3, 4), keepdims=True)
        return ((g - m) / jnp.sqrt(s + eps)).reshape(v.shape)

    def _ln_c(v, eps=1e-6):
        m = jnp.mean(v, axis=1, keepdims=True)
        s = jnp.var(v, axis=1, keepdims=True)
        return (v - m) / jnp.sqrt(s + eps)

    def _ln_t(v, eps=1e-5):
        m = jnp.mean(v, axis=-1, keepdims=True)
        s = jnp.var(v, axis=-1, keepdims=True)
        return (v - m) / jnp.sqrt(s + eps)

    def _to_tokens(v):
        B_, C_, H_, W_ = v.shape
        return v.reshape(B_, C_, H_ * W_).transpose(0, 2, 1)
    def _from_tokens(t, like):
        B_, C_, H_, W_ = like.shape
        return t.transpose(0, 2, 1).reshape(B_, C_, H_, W_)

    x = x + _L0_conv_ref(_gn(x))
    x = x + _L1_conv_ref(_gn(x), L1_conv_w1, L1_conv_w2, L1_conv_w3, L1_conv_g1, L1_conv_b1, L1_conv_m1, L1_conv_v1, L1_conv_g2, L1_conv_b2, L1_conv_m2, L1_conv_v2, L1_conv_g3, L1_conv_b3, L1_conv_m3, L1_conv_v3)
    return x


_drawn_inputs = setup_inputs


def setup_inputs(seed=0):
    import zlib

    import numpy as np

    out = dict(_drawn_inputs(seed))
    spreads = {'L1_conv_g1': (1.0, 0.2),
     'L1_conv_b1': (0.0, 0.1),
     'L1_conv_m1': (0.0, 0.1),
     'L1_conv_v1': (1.0, 0.2),
     'L1_conv_g2': (1.0, 0.2),
     'L1_conv_b2': (0.0, 0.8),
     'L1_conv_m2': (0.0, 0.8),
     'L1_conv_v2': (1.0, 0.2),
     'L1_conv_g3': (1.0, 0.2),
     'L1_conv_b3': (0.0, 0.8),
     'L1_conv_m3': (0.0, 0.8),
     'L1_conv_v3': (1.0, 0.2)}
    factors = {}
    for name, (base, spread) in spreads.items():
        noise = np.random.default_rng([zlib.crc32(name.encode()), seed]).standard_normal(out[name].shape)
        drawn = base * np.exp(spread * noise) if base else spread * noise
        out[name] = jnp.asarray(drawn.astype(out[name].dtype))
    for name, factor in factors.items():
        out[name] = (out[name] * factor).astype(out[name].dtype)
    return out
```

```python
from contextlib import ExitStack

import concourse.bass as bass
from concourse import mybir

F32 = mybir.dt.float32
F32R = mybir.dt.float32r
ALU = mybir.AluOpType
ACT = mybir.ActivationFunctionType

P = 128
SIDE = 14
S = SIDE * SIDE
C = 1024
CJ = C // P
MID = 256
MC = MID // P
ROW = CJ * S
S1 = S - P
PAD = SIDE + 2
TAPS = 9
SLOTS = 4
ZB = 4
BANKS = 4
GROUP_PARTS = 4
GN_EPS = 1e-5
BN_EPS = 1e-5
W1, W2, W3 = CJ * MID, MC * TAPS * MID, MC * C
W_EARLY = W1 + C
W_ALL = W1 + W2 + W3
BN_COLS = MC + MC + CJ
BN_LAST = 2 * MC
STAT_PIECES = 4
CONSTS = S + S1 + P


def build(nc, x, weights, bn, identity, consts, out):
    pairs = x.shape[0] // 2
    x_pairs = x.rearrange("(q s) (p j) h w -> q p s (j h w)", s=2, j=CJ)
    out_pairs = out.rearrange("(q s) (p j) h w -> q p s (j h w)", s=2, j=CJ)

    with ExitStack() as ctx:
        def sb(name, shape, dt=F32):
            return ctx.enter_context(nc.sbuf_tensor(name, shape, dt))

        def sem(name):
            return ctx.enter_context(nc.semaphore(name))

        x_ring = sb("x_ring", [P, SLOTS, 2, CJ, S])
        f_full = sb("f_full", [P, 2, CJ, S])
        scratch = sb("scratch", [P, 2, CJ, S])
        fa_hi = sb("fa_hi", [P, CJ, S], F32R)
        fa_lo = sb("fa_lo", [P, CJ, S], F32R)
        fb_hi = sb("fb_hi", [P, 2, CJ, S], F32R)
        fb_lo = sb("fb_lo", [P, 2, CJ, S], F32R)
        w_hi = sb("w_hi", [P, W_ALL], F32R)
        w_lo = sb("w_lo", [P, W_ALL], F32R)
        h1_hi = sb("h1_hi", [P, MC, 2, PAD, PAD], F32R)
        h1_lo = sb("h1_lo", [P, MC, 2, PAD, PAD], F32R)
        h2_hi = sb("h2_hi", [P, MC, 2 * S], F32R)
        h2_lo = sb("h2_lo", [P, MC, 2 * S], F32R)
        z = sb("z", [P, ZB, 2 * S])
        const = sb("const", [P, CONSTS])
        eye = sb("eye", [P, P], F32R)
        ones = sb("ones", [P, 1])
        pixel0 = sb("pixel0", [P, 2, 2], F32R)
        pixel1 = sb("pixel1", [S1, 2, 2], F32R)
        m0 = sb("m0", [P, 2])
        m1 = sb("m1", [S1, 2])
        sq0 = sb("sq0", [P, 2])
        sq1 = sb("sq1", [S1, 2])
        d0 = sb("d0", [P, 2, S])
        d1 = sb("d1", [S1, 2, S1])
        sum0 = sb("sum0", [P, 2])
        sum1 = sb("sum1", [S1, 2])
        rec0 = sb("rec0", [P, 2])
        rec1 = sb("rec1", [S1, 2])
        m_all = sb("m_all", [P, 2, S])
        pieces = [sb(f"pieces{n}", [P, 2, STAT_PIECES, 6]) for n in range(2)]
        moments = [sb(f"moments{n}", [P, 2, 2]) for n in range(2)]
        mean_sq = [sb(f"mean_sq{n}", [P, 2]) for n in range(2)]
        group = [sb(f"group{n}", [P, 2, 2]) for n in range(2)]
        var = [sb(f"var{n}", [P, 2]) for n in range(2)]
        std = [sb(f"std{n}", [P, 2]) for n in range(2)]
        rec = [sb(f"rec_std{n}", [P, 2]) for n in range(2)]
        affine1 = sb("affine1", [P, SLOTS, 2, 2])
        affine2 = sb("affine2", [P, 1, 2, 2])
        bn_in = sb("bn_in", [P, 4, BN_COLS])
        bn_std = sb("bn_std", [P, BN_COLS])
        bn_scale = sb("bn_scale", [P, BN_COLS])
        bn_shift = sb("bn_shift", [P, BN_COLS])

        conv_ps = [ctx.enter_context(nc.psum_tensor(f"conv_ps{b}", [P, 512], F32)) for b in range(BANKS)]
        gram_ps = [ctx.enter_context(nc.psum_tensor(f"gram_ps{s}", [P, 512], F32)) for s in range(2)]
        stat_ps = [ctx.enter_context(nc.psum_tensor(f"stat_ps{n}", [P, 512], F32)) for n in range(2)]

        dist0 = const[:, 0:S]
        dist1 = const[0:S1, S:S + S1]
        group_mean = const[:, S + S1:CONSTS]
        staging = x_ring[:, 2:SLOTS].rearrange("p a s j n -> p (a s j n)")
        w_raw = (scratch[:, :, :, :].rearrange("p s j n -> p (s j n)")[:, 0:W_EARLY], staging[:, 0:W_ALL - W_EARLY])
        eye_raw = staging[:, W_ALL - W_EARLY:W_ALL - W_EARLY + P]
        w_parts = (w_hi, w_lo)
        w1 = [w[:, 0:W1].rearrange("p (j o) -> p j o", j=CJ) for w in w_parts]
        w2 = [w[:, W_EARLY:W_EARLY + W2].rearrange("p (k a o) -> p k a o", k=MC, a=TAPS) for w in w_parts]
        w3 = [[w[:, at:at + C].rearrange("p (j o) -> p j o", j=CJ) for at in (W1, W_EARLY + W2)] for w in w_parts]
        w_cols = (slice(0, W_EARLY), slice(W_EARLY, W_ALL))
        fb = (fb_hi, fb_lo)
        h1 = (h1_hi, h1_lo)
        h2 = (h2_hi, h2_lo)
        PRODUCTS = ((0, 0), (0, 1), (1, 0))

        x_loaded = [sem(f"x_loaded{i}") for i in range(SLOTS)]
        stored = [sem(f"stored{i}") for i in range(SLOTS)]
        weights_loaded = [sem(f"weights_loaded{i}") for i in range(2)]
        eye_done = sem("eye_done")
        const_loaded = sem("const_loaded")
        eye_loaded = sem("eye_loaded")
        bn_loaded = sem("bn_loaded")
        fills_done = sem("fills_done")
        w_hi_done = sem("w_hi_done")
        w_lo_done = sem("w_lo_done")
        bn_std_done = sem("bn_std_done")
        bn_chain = sem("bn_chain")
        pieces_done = [sem(f"pieces_done{n}") for n in range(2)]
        moments_chain = [sem(f"moments_chain{n}") for n in range(2)]
        moments_done = [sem(f"moments_done{n}") for n in range(2)]
        group_summed = [sem(f"group_summed{n}") for n in range(2)]
        var_chain = [sem(f"var_chain{n}") for n in range(2)]
        var_done = [sem(f"var_done{n}") for n in range(2)]
        std_done = [sem(f"std_done{n}") for n in range(2)]
        scale_chain = [sem(f"scale_chain{n}") for n in range(2)]
        affine_done = [sem(f"affine_done{n}") for n in range(2)]
        f1_full = sem("f1_full")
        f1_hi = sem("f1_hi")
        f1_lo = sem("f1_lo")
        gram_done = sem("gram_done")
        diag_done = sem("diag_done")
        rows_added = sem("rows_added")
        clamped = sem("clamped")
        rooted = sem("rooted")
        damped = sem("damped")
        sums_done = sem("sums_done")
        diag_chain = sem("diag_chain")
        m_chain = sem("m_chain")
        m_split = sem("m_split")
        m_spread = sem("m_spread")
        m_done = sem("m_done")
        f1_again = sem("f1_again")
        m_f1 = sem("m_f1")
        x1_done = sem("x1_done")
        f2_full = sem("f2_full")
        f2_hi = sem("f2_hi")
        f2_lo = sem("f2_lo")
        f2_added = sem("f2_added")
        u_done = sem("u_done")
        filled = [sem(f"filled{b}") for b in range(BANKS)]
        squared = [sem(f"squared{b}") for b in range(BANKS)]
        h_affine = [sem(f"h{n}_affine") for n in (1, 2)]
        h_hi = [sem(f"h{n}_hi") for n in (1, 2)]
        h_lo = [sem(f"h{n}_lo") for n in (1, 2)]
        added = [sem(f"added{i}") for i in range(ZB)]

        def valid(j):
            return not isinstance(j, int) or 0 <= j < pairs

        def after(eng, s, value):
            if not isinstance(value, int) or value > 0:
                eng.wait_ge(s, value)

        def steps(eng, step):
            def one(q, k):
                step(SLOTS * q + k, lambda o: (k + o) % SLOTS, lambda o: q + (k + o) // SLOTS)

            for k in range(1, SLOTS):
                one(-1, k)
            whole = pairs // SLOTS - 1
            if whole > 0:
                with eng.Fori(0, whole) as q:
                    for k in range(SLOTS):
                        one(q, k)
            for k in range(SLOTS):
                one(whole, k)

        block = ctx.enter_context(nc.Block())

        @block.sync
        def _(sp):
            sp.dma_start(x_ring[:, 0].rearrange("p s j n -> p s (j n)"), x_pairs[0]).then_inc(x_loaded[0], 16)
            sp.dma_start(bn_in[:, :, :], bn).then_inc(bn_loaded, 16)
            sp.dma_start(const[:, :], consts).then_inc(const_loaded, 16)
            sp.dma_start(eye_raw, identity).then_inc(eye_loaded, 16)
            sp.dma_start(w_raw[0], weights[:, 0:W_EARLY]).then_inc(weights_loaded[0], 16)
            sp.dma_start(x_ring[:, 1].rearrange("p s j n -> p s (j n)"), x_pairs[1]).then_inc(x_loaded[1], 16)
            sp.dma_start(w_raw[1], weights[:, W_EARLY:]).then_inc(weights_loaded[1], 16)
            sp.wait_ge(eye_done, 1)
            sp.wait_ge(w_lo_done, 2)
            sp.dma_start(x_ring[:, 2].rearrange("p s j n -> p s (j n)"), x_pairs[2]).then_inc(x_loaded[2], 16)

            def step(t, slot, visit):
                if isinstance(t, int) and t < 0:
                    return
                if valid(t + 3):
                    after(sp, stored[slot(3)], 16 * visit(3))
                    sp.dma_start(x_ring[:, slot(3)].rearrange("p s j n -> p s (j n)"),
                                 x_pairs[bass.ds(t + 3, 1)].rearrange("q p s n -> (q p) s n")
                                 ).then_inc(x_loaded[slot(3)], 16)
                for i in range(ZB):
                    sp.wait_ge(added[i], 2 * t + 2)
                sp.dma_start(out_pairs[bass.ds(t, 1)].rearrange("q p s n -> (q p) s n"),
                             x_ring[:, slot(0)].rearrange("p s j n -> p s (j n)")).then_inc(stored[slot(0)], 16)

            steps(sp, step)
            for i in range(SLOTS):
                sp.wait_ge(stored[i], 16 * (pairs // SLOTS))

        @block.gpsimd
        def _(pool):
            nc.gpsimd.memset(ones[:, :], 1.0)
            nc.gpsimd.memset(h1_hi[:, :, :, :, :].bitcast(F32), 0.0)
            nc.gpsimd.memset(h1_lo[:, :, :, :, :].bitcast(F32), 0.0).then_inc(fills_done, 1)
            for i in range(2):
                pool.wait_ge(w_hi_done, i + 1)
                nc.gpsimd.tensor_tensor(w_lo[:, w_cols[i]], w_raw[i], w_hi[:, w_cols[i]].bitcast(F32), ALU.subtract
                                        ).then_inc(w_lo_done, 1)
            pool.wait_ge(bn_chain, 9)

            def step(t, slot, visit):
                b = t + 1
                if not valid(b):
                    return
                for s in range(2):
                    n = 2 * b + s
                    at = x_ring[:, slot(1), s]
                    pool.wait_ge(f1_again, n + 1)
                    pool.wait_ge(m_done, n + 1)
                    nc.gpsimd.tensor_tensor(scratch[:, s], scratch[:, s],
                                            m_all[:, s].unsqueeze(1).to_broadcast([P, CJ, S]),
                                            ALU.mult).then_inc(m_f1, 1)
                    pool.wait_ge(m_f1, n + 1)
                    nc.gpsimd.tensor_tensor(at, scratch[:, s], at, ALU.add).then_inc(x1_done, 1)
                for s in range(2):
                    n = 2 * b + s
                    at = x_ring[:, slot(1), s]
                    pool.wait_ge(f2_full, n + 1)
                    pool.wait_ge(pieces_done[1], n + 1)
                    nc.gpsimd.tensor_tensor(at, at, f_full[:, s], ALU.add).then_inc(f2_added, 1)
                    pool.wait_ge(f2_added, n + 1)
                    nc.gpsimd.tensor_tensor(at, at, bn_shift[:, BN_LAST:].unsqueeze(2).to_broadcast([P, CJ, S]),
                                            ALU.add).then_inc(u_done, 1)

            steps(pool, step)

        @block.scalar
        def _(act):
            act.wait_ge(bn_loaded, 16)
            act.wait_ge(bn_chain, 1)
            nc.scalar.activation(bn_std[:, :], bn_in[:, 3, :], ACT.Sqrt).then_inc(bn_std_done, 1)

            def w_hi_of(i):
                act.wait_ge(weights_loaded[i], 16)
                nc.scalar.activation(w_hi[:, w_cols[i]], w_raw[i], ACT.Copy).then_inc(w_hi_done, 1)


            def root_var(n, j):
                act.wait_ge(var_done[n], j + 1)
                nc.scalar.activation(std[n][:, :], var[n][:, :], ACT.Sqrt).then_inc(std_done[n], 1)

            def f1_of(j, s, slot):
                act.wait_ge(affine_done[0], j + 1)
                after(act, f2_added, 2 * j + s - 3)
                nc.scalar.activation(f_full[:, s], x_ring[:, slot, s], ACT.Identity,
                                     bias=affine1[:, slot, s, 1:2], scale=affine1[:, slot, s, 0:1]
                                     ).then_inc(f1_full, 1)

            def f1_again_of(j, s, slot):
                if isinstance(j, int) and j == 0:
                    act.wait_ge(w_lo_done, 1)
                after(act, x1_done, 2 * j + s - 1)
                nc.scalar.activation(scratch[:, s], x_ring[:, slot, s], ACT.Identity,
                                     bias=affine1[:, slot, s, 1:2], scale=affine1[:, slot, s, 0:1]
                                     ).then_inc(f1_again, 1)

            def f1_hi_of(j, s):
                act.wait_ge(f1_full, 2 * j + s + 1)
                after(act, gram_done, 2 * j + s)
                nc.scalar.activation(fa_hi[:, :, :], f_full[:, s], ACT.Copy).then_inc(f1_hi, 1)

            def f2_of(j, s, slot):
                act.wait_ge(affine_done[1], j + 1)
                if valid(j + 1):
                    act.wait_ge(f1_lo, 2 * j + s + 3)
                nc.scalar.activation(f_full[:, s], x_ring[:, slot, s], ACT.Identity,
                                     bias=affine2[:, 0, s, 1:2], scale=affine2[:, 0, s, 0:1]
                                     ).then_inc(f2_full, 1)

            def f2_hi_of(j, s):
                act.wait_ge(f2_full, 2 * j + s + 1)
                after(act, filled[1], 3 * j - 2)
                nc.scalar.activation(fb_hi[:, s], f_full[:, s], ACT.Copy).then_inc(f2_hi, 1)

            def root_d(j, s):
                act.wait_ge(clamped, 2 * j + s + 1)
                nc.scalar.activation(d0[:, s], d0[:, s], ACT.Sqrt, bias=sq0[:, s:s + 1], scale=-1.0)
                nc.scalar.activation(d1[:, s], d1[:, s], ACT.Sqrt, bias=sq1[:, s:s + 1], scale=-1.0
                                     ).then_inc(rooted, 1)

            def m_of(j, s):
                act.wait_ge(m_spread, 2 * j + s + 1)
                after(act, m_f1, 2 * j + s - 1)
                nc.scalar.activation(m_all[:, s], gram_ps[s][:, 0:S], ACT.Copy).then_inc(m_done, 1)

            def square(t, layer, m):
                bank = 2 * layer + m
                if layer == 0:
                    act.wait_ge(added[m], 2 * t)
                act.wait_ge(filled[bank], 3 * t + 1)
                nc.scalar.activation(z[:, m], conv_ps[bank][:, 0:2 * S], ACT.Square, bias=1.0
                                     ).then_inc(squared[bank], 1)

            def h_hi_of(t, layer, m):
                act.wait_ge(h_affine[layer], 2 * t + m + 1)
                if layer == 0:
                    nc.scalar.activation(h1_hi[:, m, :, 1:1 + SIDE, 1:1 + SIDE],
                                         z[:, m].rearrange("p (s h w) -> p s h w", s=2, h=SIDE), ACT.Copy
                                         ).then_inc(h_hi[0], 1)
                else:
                    nc.scalar.activation(h2_hi[:, m], z[:, m], ACT.Copy).then_inc(h_hi[1], 1)

            def square_last(t, j):
                bank, buf = j % BANKS, (j + MC) % ZB
                act.wait_ge(filled[bank], 3 * t + 2 + j // BANKS)
                act.wait_ge(added[buf], 2 * t + j // ZB)
                nc.scalar.activation(z[:, buf], conv_ps[bank][:, 0:2 * S], ACT.Square, bias=1.0
                                     ).then_inc(squared[bank], 1)

            def step(t, slot, visit):
                a, b, c = valid(t + 2), valid(t + 1), valid(t)
                if isinstance(t, int) and t == -3:
                    w_hi_of(0)
                if a:
                    f1_hi_of(t + 2, 0)
                if c:
                    square(t, 0, 0)
                    h_hi_of(t, 0, 0)
                if b:
                    m_of(t + 1, 1)
                if a:
                    f1_of(t + 2, 1, slot(2))
                if c:
                    square(t, 0, 1)
                    h_hi_of(t, 0, 1)
                if a:
                    f1_hi_of(t + 2, 1)
                    f1_again_of(t + 2, 0, slot(2))
                    f1_again_of(t + 2, 1, slot(2))
                    root_d(t + 2, 0)
                if c:
                    square(t, 1, 0)
                if b:
                    root_var(1, t + 1)
                if c:
                    h_hi_of(t, 1, 0)
                if b:
                    f2_of(t + 1, 0, slot(1))
                    f2_hi_of(t + 1, 0)
                    f2_of(t + 1, 1, slot(1))
                    f2_hi_of(t + 1, 1)
                if c:
                    square(t, 1, 1)
                    h_hi_of(t, 1, 1)
                if valid(t + 3):
                    root_var(0, t + 3)
                if c:
                    for j in range(0, 3):
                        square_last(t, j)
                if a:
                    root_d(t + 2, 1)
                if c:
                    for j in range(3, 6):
                        square_last(t, j)
                if a:
                    m_of(t + 2, 0)
                if c:
                    for j in range(6, 8):
                        square_last(t, j)
                if valid(t + 3):
                    f1_of(t + 3, 0, slot(3))
                if isinstance(t, int) and t == -3:
                    w_hi_of(1)

            steps(act, step)

        @block.vector
        def _(dve):
            dve.wait_ge(bn_loaded, 16)
            nc.vector.tensor_scalar_add(bn_in[:, 3, :], bn_in[:, 3, :], BN_EPS).then_inc(bn_chain, 1)
            dve.wait_ge(bn_std_done, 1)
            nc.vector.reciprocal(bn_std[:, :], bn_std[:, :]).then_inc(bn_chain, 1)
            dve.wait_ge(bn_chain, 2)
            nc.vector.tensor_tensor(bn_scale[:, :], bn_in[:, 3, :], bn_std[:, :], ALU.mult).then_inc(bn_chain, 1)
            dve.wait_ge(bn_chain, 3)
            nc.vector.tensor_tensor(bn_scale[:, :], bn_scale[:, :], bn_std[:, :], ALU.mult).then_inc(bn_chain, 1)
            dve.wait_ge(bn_chain, 4)
            nc.vector.tensor_scalar(bn_scale[:, :], bn_scale[:, :], -0.5, 1.5, ALU.mult, ALU.add).then_inc(bn_chain, 1)
            dve.wait_ge(bn_chain, 5)
            nc.vector.tensor_tensor(bn_std[:, :], bn_scale[:, :], bn_std[:, :], ALU.mult).then_inc(bn_chain, 1)
            dve.wait_ge(bn_chain, 6)
            nc.vector.tensor_tensor(bn_scale[:, :], bn_in[:, 0, :], bn_std[:, :], ALU.mult).then_inc(bn_chain, 1)
            dve.wait_ge(bn_chain, 7)
            nc.vector.tensor_tensor(bn_shift[:, :], bn_in[:, 2, :], bn_scale[:, :], ALU.mult).then_inc(bn_chain, 1)
            dve.wait_ge(bn_chain, 8)
            nc.vector.tensor_tensor(bn_shift[:, :], bn_in[:, 1, :], bn_shift[:, :], ALU.subtract).then_inc(bn_chain, 1)
            dve.wait_ge(bn_chain, 9)
            dve.wait_ge(eye_loaded, 16)
            nc.vector.tensor_copy(eye[:, :], eye_raw).then_inc(eye_done, 1)
            dve.wait_ge(const_loaded, 16)

            def stat_pieces(n, j, s, slot):
                row = x_ring[:, slot, s].rearrange("p (a j) n -> p a (j n)", a=STAT_PIECES)
                for a in range(STAT_PIECES):
                    last = nc.vector.bn_stats(pieces[n][:, s, a, :], row[:, a])
                last.then_inc(pieces_done[n], 1)

            def moments_of(n, j):
                dve.wait_ge(pieces_done[n], 2 * j + 2)
                nc.vector.tensor_copy(mean_sq[n][:, 0:1], pieces[n][:, 1, 0, 0:1])
                for s in range(2):
                    last = nc.vector.bn_aggr(moments[n][:, s, :], pieces[n][:, s].rearrange("p a e -> p (a e)"))
                last.then_inc(moments_chain[n], 1)
                dve.wait_ge(moments_chain[n], 2 * j + 1)
                nc.vector.tensor_tensor(mean_sq[n][:, :], moments[n][:, :, 0], moments[n][:, :, 0], ALU.mult
                                        ).then_inc(moments_chain[n], 1)
                dve.wait_ge(moments_chain[n], 2 * j + 2)
                nc.vector.tensor_tensor(moments[n][:, :, 1], moments[n][:, :, 1], mean_sq[n][:, :], ALU.add
                                        ).then_inc(moments_done[n], 1)

            def group_var(n, j):
                dve.wait_ge(group_summed[n], j + 1)
                nc.vector.tensor_copy(group[n][:, :, :].rearrange("p s e -> p (s e)"), stat_ps[n][:, 0:4]
                                      ).then_inc(var_chain[n], 1)
                dve.wait_ge(var_chain[n], 3 * j + 1)
                nc.vector.tensor_tensor(mean_sq[n][:, :], group[n][:, :, 0], group[n][:, :, 0], ALU.mult
                                        ).then_inc(var_chain[n], 1)
                dve.wait_ge(var_chain[n], 3 * j + 2)
                nc.vector.tensor_tensor(var[n][:, :], group[n][:, :, 1], mean_sq[n][:, :], ALU.subtract
                                        ).then_inc(var_chain[n], 1)
                dve.wait_ge(var_chain[n], 3 * j + 3)
                nc.vector.tensor_scalar(var[n][:, :], var[n][:, :], 0.0, GN_EPS, ALU.max, ALU.add
                                        ).then_inc(var_done[n], 1)

            def affine_of(n, j, to):
                dve.wait_ge(std_done[n], j + 1)
                nc.vector.reciprocal(rec[n][:, :], std[n][:, :]).then_inc(scale_chain[n], 1)
                dve.wait_ge(scale_chain[n], 5 * j + 1)
                nc.vector.tensor_tensor(mean_sq[n][:, :], var[n][:, :], rec[n][:, :], ALU.mult
                                        ).then_inc(scale_chain[n], 1)
                dve.wait_ge(scale_chain[n], 5 * j + 2)
                nc.vector.tensor_tensor(mean_sq[n][:, :], mean_sq[n][:, :], rec[n][:, :], ALU.mult
                                        ).then_inc(scale_chain[n], 1)
                dve.wait_ge(scale_chain[n], 5 * j + 3)
                nc.vector.tensor_scalar(mean_sq[n][:, :], mean_sq[n][:, :], -0.5, 1.5, ALU.mult, ALU.add
                                        ).then_inc(scale_chain[n], 1)
                dve.wait_ge(scale_chain[n], 5 * j + 4)
                nc.vector.tensor_tensor(to[:, :, 0], mean_sq[n][:, :], rec[n][:, :], ALU.mult
                                        ).then_inc(scale_chain[n], 1)
                dve.wait_ge(scale_chain[n], 5 * j + 5)
                nc.vector.scalar_tensor_tensor(to[:, :, 1], group[n][:, :, 0], -1.0, to[:, :, 0],
                                               ALU.mult, ALU.mult).then_inc(affine_done[n], 1)

            def f1_lo_of(j, s):
                dve.wait_ge(f1_hi, 2 * j + s + 1)
                nc.vector.tensor_tensor(fa_lo[:, :, :], f_full[:, s], fa_hi[:, :, :].bitcast(F32), ALU.subtract
                                        ).then_inc(f1_lo, 1)

            def f2_lo_of(j, s):
                dve.wait_ge(f2_hi, 2 * j + s + 1)
                nc.vector.tensor_tensor(fb_lo[:, s], f_full[:, s], fb_hi[:, s].bitcast(F32), ALU.subtract
                                        ).then_inc(f2_lo, 1)

            def diag_of(j, s):
                n = 2 * j + s
                dve.wait_ge(gram_done, n + 1)
                nc.vector.tensor_tensor_reduce(out=d0[:, s, 0:P], in0=gram_ps[s][:, 0:P], in1=eye[:, :].bitcast(F32),
                                               scale=1.0, scalar=0.0, op0=ALU.mult, op1=ALU.add,
                                               accum_out=sq0[:, s:s + 1])
                nc.vector.tensor_tensor_reduce(out=d1[:, s], in0=gram_ps[s][0:S1, S:S + S1],
                                               in1=eye[0:S1, 0:S1].bitcast(F32),
                                               scale=1.0, scalar=0.0, op0=ALU.mult, op1=ALU.add,
                                               accum_out=sq1[:, s:s + 1]).then_inc(diag_chain, 1)
                dve.wait_ge(diag_chain, 2 * n + 1)
                nc.vector.tensor_scalar(pixel0[:, s, 0:1], sq0[:, s:s + 1], -0.5, None, ALU.mult)
                nc.vector.tensor_scalar(pixel1[:, s, 0:1], sq1[:, s:s + 1], -0.5, None, ALU.mult
                                        ).then_inc(diag_chain, 1)
                dve.wait_ge(diag_chain, 2 * n + 2)
                nc.vector.scalar_tensor_tensor(pixel0[:, s, 1:2], sq0[:, s:s + 1], -0.5,
                                               pixel0[:, s, 0:1].bitcast(F32), ALU.mult, ALU.subtract)
                nc.vector.scalar_tensor_tensor(pixel1[:, s, 1:2], sq1[:, s:s + 1], -0.5,
                                               pixel1[:, s, 0:1].bitcast(F32), ALU.mult, ALU.subtract
                                               ).then_inc(diag_done, 1)

            def clamp(j, s):
                dve.wait_ge(rows_added, 2 * j + s + 1)
                nc.vector.tensor_scalar(d0[:, s], gram_ps[s][:, 0:S], 2.0, sq0[:, s:s + 1], ALU.mult, ALU.min)
                nc.vector.tensor_scalar(d1[:, s], gram_ps[s][0:S1, S:S + S1], 2.0, sq1[:, s:s + 1],
                                        ALU.mult, ALU.min).then_inc(clamped, 1)

            def damp(j, s):
                dve.wait_ge(rooted, 2 * j + s + 1)
                nc.vector.tensor_tensor_reduce(out=d0[:, s], in0=d0[:, s], in1=dist0, scale=1.0, scalar=0.0,
                                               op0=ALU.mult, op1=ALU.add, accum_out=sum0[:, s:s + 1])
                nc.vector.tensor_tensor(d1[:, s], d1[:, s], dist1, ALU.mult).then_inc(damped, 1)

            def new_m(j, s):
                n = 2 * j + s
                dve.wait_ge(sums_done, n + 1)
                nc.vector.tensor_copy(sum1[:, s:s + 1], gram_ps[s][0:S1, S:S + 1])
                nc.vector.reciprocal(rec0[:, s:s + 1], sum0[:, s:s + 1]).then_inc(m_chain, 1)
                dve.wait_ge(m_chain, 3 * n + 1)
                nc.vector.reciprocal(rec1[:, s:s + 1], sum1[:, s:s + 1]).then_inc(m_chain, 1)
                dve.wait_ge(m_chain, 3 * n + 2)
                for to in (m0[:, s:s + 1], pixel0[:, s, 0:1]):
                    nc.vector.tensor_scalar(to, sum0[:, s:s + 1], 1.0 / S, rec0[:, s:s + 1], ALU.mult, ALU.mult)
                for to in (m1[:, s:s + 1], pixel1[:, s, 0:1]):
                    last = nc.vector.tensor_scalar(to, sum1[:, s:s + 1], 1.0 / S, rec1[:, s:s + 1],
                                                   ALU.mult, ALU.mult)
                last.then_inc(m_chain, 1)
                dve.wait_ge(m_chain, 3 * n + 3)
                nc.vector.tensor_tensor(pixel0[:, s, 1:2], m0[:, s:s + 1], pixel0[:, s, 0:1].bitcast(F32),
                                        ALU.subtract)
                nc.vector.tensor_tensor(pixel1[:, s, 1:2], m1[:, s:s + 1], pixel1[:, s, 0:1].bitcast(F32),
                                        ALU.subtract).then_inc(m_split, 1)

            def h_affine_of(t, layer, m):
                col = MC * layer + m
                dve.wait_ge(squared[2 * layer + m], 3 * t + 1)
                nc.vector.tensor_scalar(z[:, m], z[:, m], bn_scale[:, col:col + 1], bn_shift[:, col:col + 1],
                                        ALU.mult, ALU.add).then_inc(h_affine[layer], 1)

            def h_lo_of(t, layer, m):
                dve.wait_ge(h_hi[layer], 2 * t + m + 1)
                if layer == 0:
                    inner = (slice(None), m, slice(None), slice(1, 1 + SIDE), slice(1, 1 + SIDE))
                    nc.vector.tensor_tensor(h1_lo[inner], z[:, m].rearrange("p (s h w) -> p s h w", s=2, h=SIDE),
                                            h1_hi[inner].bitcast(F32), ALU.subtract).then_inc(h_lo[0], 1)
                else:
                    nc.vector.tensor_tensor(h2_lo[:, m], z[:, m], h2_hi[:, m].bitcast(F32), ALU.subtract
                                            ).then_inc(h_lo[1], 1)

            def add_last(t, j, slot):
                if j == 0:
                    dve.wait_ge(u_done, 2 * t + 2)
                dve.wait_ge(squared[j % BANKS], 3 * t + 2 + j // BANKS)
                at, buf = x_ring[:, slot, :, j], (j + MC) % ZB
                nc.vector.scalar_tensor_tensor(at, z[:, buf].rearrange("p (s n) -> p s n", s=2),
                                               bn_scale[:, BN_LAST + j:BN_LAST + j + 1], at,
                                               ALU.mult, ALU.add).then_inc(added[buf], 1)

            def step(t, slot, visit):
                a, b, c, e = valid(t + 2), valid(t + 1), valid(t), valid(t + 3)
                if b:
                    new_m(t + 1, 1)
                if a:
                    f1_lo_of(t + 2, 0)
                if c:
                    h_affine_of(t, 0, 0)
                    h_lo_of(t, 0, 0)
                if b:
                    dve.wait_ge(x1_done, 2 * (t + 1) + 1)
                    stat_pieces(1, t + 1, 0, slot(1))
                if c:
                    h_affine_of(t, 0, 1)
                    h_lo_of(t, 0, 1)
                if a:
                    diag_of(t + 2, 0)
                    f1_lo_of(t + 2, 1)
                if b:
                    dve.wait_ge(x1_done, 2 * (t + 1) + 2)
                    stat_pieces(1, t + 1, 1, slot(1))
                    moments_of(1, t + 1)
                if a:
                    clamp(t + 2, 0)
                if b:
                    group_var(1, t + 1)
                if c:
                    h_affine_of(t, 1, 0)
                if b:
                    affine_of(1, t + 1, affine2[:, 0])
                if a:
                    damp(t + 2, 0)
                if e:
                    dve.wait_ge(x_loaded[slot(3)], 16 * visit(3) + 16)
                    stat_pieces(0, t + 3, 0, slot(3))
                if c:
                    h_lo_of(t, 1, 0)
                if e:
                    stat_pieces(0, t + 3, 1, slot(3))
                    moments_of(0, t + 3)
                if b:
                    f2_lo_of(t + 1, 0)
                if c:
                    h_affine_of(t, 1, 1)
                if e:
                    group_var(0, t + 3)
                if c:
                    h_lo_of(t, 1, 1)
                if e:
                    affine_of(0, t + 3, affine1[:, slot(3)])
                if b:
                    f2_lo_of(t + 1, 1)
                if a:
                    diag_of(t + 2, 1)
                if c:
                    add_last(t, 0, slot(0))
                if a:
                    new_m(t + 2, 0)
                if c:
                    add_last(t, 1, slot(0))
                if a:
                    clamp(t + 2, 1)
                if c:
                    for j in range(2, 5):
                        add_last(t, j, slot(0))
                if a:
                    damp(t + 2, 1)
                if c:
                    for j in range(5, 8):
                        add_last(t, j, slot(0))

            steps(dve, step)

        @block.tensor
        def _(pe):
            pe.wait_ge(const_loaded, 16)
            pe.wait_ge(eye_done, 1)

            def gram(j, s):
                n = 2 * j + s
                after(pe, m_done, n - 1)
                pe.wait_ge(f1_lo, n + 1)
                parts = (fa_hi, fa_lo)
                for c in range(CJ):
                    for i, (w, m) in enumerate(PRODUCTS):
                        nc.tensor.matmul(gram_ps[s][:, 0:S], parts[w][:, c, 0:P], parts[m][:, c, :],
                                         start=(c == 0 and i == 0), stop=False, skip_group_check=True)
                for c in range(CJ):
                    for i, (w, m) in enumerate(PRODUCTS):
                        last = nc.tensor.matmul(gram_ps[s][0:S1, S:S + S1], parts[w][:, c, P:S], parts[m][:, c, P:S],
                                                start=False, stop=(c == CJ - 1 and i == 2), skip_group_check=True)
                last.then_inc(gram_done, 1)

            def spread_pixels(s, other_rows, start):
                for i in range(2):
                    of0 = pixel0[:, s, i:i + 1].to_broadcast([P, P])
                    of1 = pixel1[:, s, i:i + 1].to_broadcast([S1, P])
                    nc.tensor.matmul(gram_ps[s][:, 0:P], of0, eye[:, :], start=start and i == 0, stop=False,
                                     skip_group_check=True)
                    last = nc.tensor.matmul(gram_ps[s][:, P:S], of1, eye[0:S1, 0:S1], start=False, stop=i == 1,
                                            skip_group_check=True)
                    if other_rows:
                        last = nc.tensor.matmul(gram_ps[s][0:S1, S:S + S1], pixel1[:, s, i:i + 1].to_broadcast([S1, S1]),
                                                eye[0:S1, 0:S1], start=False, stop=i == 1, skip_group_check=True)
                return last

            def add_rows(j, s):
                pe.wait_ge(diag_done, 2 * j + s + 1)
                spread_pixels(s, other_rows=True, start=False).then_inc(rows_added, 1)

            def sum_rows(j, s):
                pe.wait_ge(damped, 2 * j + s + 1)
                nc.tensor.matmul(gram_ps[s][0:S1, S:S + 1], d0[:, s, P:S], ones[:, :], start=True, stop=False)
                nc.tensor.matmul(gram_ps[s][0:S1, S:S + 1], d1[:, s], ones[0:S1, :], start=False, stop=True
                                 ).then_inc(sums_done, 1)

            def spread_m(j, s):
                pe.wait_ge(m_split, 2 * j + s + 1)
                spread_pixels(s, other_rows=False, start=True).then_inc(m_spread, 1)

            def sum_group(n, j):
                pe.wait_ge(moments_done[n], j + 1)
                nc.tensor.matmul(stat_ps[n][:, 0:4], group_mean, moments[n][:, :, :].rearrange("p s e -> p (s e)"),
                                 start=True, stop=True).then_inc(group_summed[n], 1)

            def conv1(t, m):
                if isinstance(t, int) and t == 0 and m == 0:
                    pe.wait_ge(fills_done, 1)
                    pe.wait_ge(w_lo_done, 2)
                if m == 0:
                    pe.wait_ge(f2_lo, 2 * t + 2)
                pe.wait_ge(squared[m], 3 * t)
                for j in range(CJ):
                    for i, (w, f) in enumerate(PRODUCTS):
                        last = nc.tensor.matmul(conv_ps[m][:, 0:2 * S], w1[w][:, j, m * P:(m + 1) * P],
                                                fb[f][:, :, j], start=(j == 0 and i == 0),
                                                stop=(j == CJ - 1 and i == 2))
                last.then_inc(filled[m], 1)

            def conv2(t, m, inputs=range(MC)):
                bank = 2 + m
                if 0 in inputs:
                    pe.wait_ge(squared[bank], 3 * t)
                for k in inputs:
                    if m == 0:
                        pe.wait_ge(h_lo[0], 2 * t + k + 1)
                    for dy in (1, 0, 2):
                        top, bottom = max(1 - dy, 0), SIDE - max(dy - 1, 0)
                        to = conv_ps[bank][:, 0:2 * S].rearrange("p (s n) -> p s n", s=2)[
                            :, :, top * SIDE:bottom * SIDE]
                        for dx in range(3):
                            for i, (w, f) in enumerate(PRODUCTS):
                                last = nc.tensor.matmul(to, w2[w][:, k, 3 * dy + dx, m * P:(m + 1) * P],
                                                        h1[f][:, k, :, top + dy:bottom + dy, dx:dx + SIDE],
                                                        start=(k == 0 and dy == 1 and dx == 0 and i == 0),
                                                        stop=(k == MC - 1 and dy == 2 and dx == 2 and i == 2))
                if MC - 1 in inputs:
                    last.then_inc(filled[bank], 1)

            def conv3(t, j):
                bank = j % BANKS
                if j == 0:
                    pe.wait_ge(h_lo[1], 2 * t + 2)
                pe.wait_ge(squared[bank], 3 * t + 1 + j // BANKS)
                for k in range(MC):
                    for i, (w, f) in enumerate(PRODUCTS):
                        last = nc.tensor.matmul(conv_ps[bank][:, 0:2 * S], w3[w][k][:, j], h2[f][:, k],
                                                start=(k == 0 and i == 0), stop=(k == MC - 1 and i == 2))
                last.then_inc(filled[bank], 1)

            def step(t):
                a, b, c, e = valid(t + 2), valid(t + 1), valid(t), valid(t + 3)
                if c:
                    conv1(t, 0)
                if b:
                    spread_m(t + 1, 1)
                if c:
                    conv1(t, 1)
                if a:
                    gram(t + 2, 0)
                if c:
                    conv2(t, 0, inputs=[0])
                if a:
                    add_rows(t + 2, 0)
                if c:
                    conv2(t, 0, inputs=[1])
                if b:
                    sum_group(1, t + 1)
                if c:
                    conv2(t, 1)
                if e:
                    sum_group(0, t + 3)
                if a:
                    sum_rows(t + 2, 0)
                    gram(t + 2, 1)
                if c:
                    for j in range(0, 2):
                        conv3(t, j)
                if a:
                    add_rows(t + 2, 1)
                if c:
                    for j in range(2, 6):
                        conv3(t, j)
                if a:
                    spread_m(t + 2, 0)
                if c:
                    for j in range(6, 8):
                        conv3(t, j)
                if a:
                    sum_rows(t + 2, 1)

            for t in range(-3, 1):
                step(t)
            if pairs > 4:
                with pe.Fori(1, pairs - 3) as t:
                    step(t)
            for t in range(max(pairs - 3, 0), pairs):
                step(t)


def constants():
    import numpy as np

    at = np.stack(np.meshgrid(np.arange(SIDE), np.arange(SIDE), indexing="ij")).reshape(2, -1)
    d2 = ((at[:, :, None] - at[:, None, :]) ** 2).sum(0).astype(np.float32)
    dist = np.exp(-d2 / np.float32(2.0 * (0.15 * SIDE) ** 2)).astype(np.float32)
    table = np.zeros((P, CONSTS), np.float32)
    table[:, 0:S] = dist[0:P]
    table[0:S1, S:S + S1] = dist[P:, P:]
    p = np.arange(P) // GROUP_PARTS
    table[:, S + S1:] = (p[:, None] == p[None, :]) / np.float32(GROUP_PARTS)
    return table


def laid_out(inputs):
    import numpy as np

    a = {k: np.asarray(v) for k, v in inputs.items()}
    w1 = a["L1_conv_w1"].reshape(MID, P, CJ).transpose(1, 2, 0).reshape(P, W1)
    w2 = a["L1_conv_w2"].reshape(MID, MC, P, TAPS).transpose(2, 1, 3, 0).reshape(P, W2)
    w3 = a["L1_conv_w3"].reshape(P, CJ, MC, P).transpose(3, 2, 1, 0).reshape(P, MC, C)
    bn = []
    for what in "gbmv":
        cols = [a[f"L1_conv_{what}{i}"].reshape(MC, P).T for i in (1, 2)]
        bn.append(np.concatenate(cols + [a[f"L1_conv_{what}3"].reshape(P, CJ)], axis=1))
    return {
        "x": np.ascontiguousarray(a["x"]),
        "weights": np.ascontiguousarray(np.concatenate([w1, w3[:, 0], w2, w3[:, 1]], axis=1)),
        "bn": np.ascontiguousarray(np.stack(bn, axis=1)),
        "identity": np.eye(P, dtype=np.float32),
        "consts": constants(),
    }


def kernel(**inputs):
    import concourse.bacc as bacc
    from concourse.bass_utils import run_bass_kernel_spmd

    nc = bacc.Bacc("TRN2", target_bir_lowering=False, num_devices=1)
    arrays = laid_out(inputs)
    args = [nc.dram_tensor(n, v.shape, F32, kind="ExternalInput").ap() for n, v in arrays.items()]
    out = nc.dram_tensor("out", arrays["x"].shape, F32, kind="ExternalOutput").ap()
    build(nc, *args, out)
    r = run_bass_kernel_spmd(nc, [arrays], core_ids=[0])
    return r.results[0]["out"]
```

```python
from contextlib import ExitStack

import concourse.bass as bass
from concourse import mybir

F32 = mybir.dt.float32
F32R = mybir.dt.float32r
ALU = mybir.AluOpType
ACT = mybir.ActivationFunctionType

P = 128
SIDE = 14
S = SIDE * SIDE
C = 1024
CJ = C // P
MID = 256
MC = MID // P
ROW = CJ * S
S1 = S - P
PAD = SIDE + 2
TAPS = 9
SLOTS = 4
ZB = 4
BANKS = 4
GROUP_PARTS = 4
GN_EPS = 1e-5
BN_EPS = 1e-5
W1, W2, W3 = CJ * MID, MC * TAPS * MID, MC * C
W_EARLY = W1 + C
W_ALL = W1 + W2 + W3
BN_COLS = MC + MC + CJ
BN_LAST = 2 * MC
STAT_PIECES = 4
HALVES = (slice(0, CJ // 2), slice(CJ // 2, CJ))
CONSTS = S + S1 + P


def build(nc, x, weights, bn, identity, consts, out):
    pairs = x.shape[0] // 2
    x_pairs = x.rearrange("(q s) (p j) h w -> q p s (j h w)", s=2, j=CJ)
    out_pairs = out.rearrange("(q s) (p j) h w -> q p s (j h w)", s=2, j=CJ)

    with ExitStack() as ctx:
        def sb(name, shape, dt=F32):
            return ctx.enter_context(nc.sbuf_tensor(name, shape, dt))

        def sem(name):
            return ctx.enter_context(nc.semaphore(name))

        x_ring = sb("x_ring", [P, SLOTS, 2, CJ, S])
        f_full = sb("f_full", [P, 2, CJ, S])
        scratch = sb("scratch", [P, 2, CJ, S])
        fa = sb("fa", [P, CJ, 2, S], F32R)
        fb_hi = sb("fb_hi", [P, 2, CJ, S], F32R)
        fb_lo = sb("fb_lo", [P, 2, CJ, S], F32R)
        w_hi = sb("w_hi", [P, W_ALL], F32R)
        w_lo = sb("w_lo", [P, W_ALL], F32R)
        h1_hi = sb("h1_hi", [P, MC, PAD, PAD, 2], F32R)
        h1_lo = sb("h1_lo", [P, MC, PAD, PAD, 2], F32R)
        h2_hi = sb("h2_hi", [P, MC, 2 * S], F32R)
        h2_lo = sb("h2_lo", [P, MC, 2 * S], F32R)
        z = sb("z", [P, ZB, 2 * S])
        const = sb("const", [P, CONSTS])
        eye = sb("eye", [P, P], F32R)
        ones = sb("ones", [P, 1])
        pixel0 = sb("pixel0", [P, 2, 2], F32R)
        pixel1 = sb("pixel1", [S1, 2, 2], F32R)
        m0 = sb("m0", [P, 2])
        m1 = sb("m1", [S1, 2])
        sq0 = sb("sq0", [P, 2])
        sq1 = sb("sq1", [S1, 2])
        d0 = sb("d0", [P, 2, S])
        d1 = sb("d1", [S1, 2, S1])
        sum0 = sb("sum0", [P, 2])
        sum1 = sb("sum1", [S1, 2])
        rec0 = sb("rec0", [P, 2])
        rec1 = sb("rec1", [S1, 2])
        m_all = sb("m_all", [P, 2, S])
        pieces = [sb(f"pieces{n}", [P, 2, STAT_PIECES, 6]) for n in range(2)]
        moments = [sb(f"moments{n}", [P, 2, 2]) for n in range(2)]
        mean_sq = [sb(f"mean_sq{n}", [P, 2]) for n in range(2)]
        group = [sb(f"group{n}", [P, 2, 2]) for n in range(2)]
        var = [sb(f"var{n}", [P, 2]) for n in range(2)]
        std = [sb(f"std{n}", [P, 2]) for n in range(2)]
        rec = [sb(f"rec_std{n}", [P, 2]) for n in range(2)]
        affine1 = sb("affine1", [P, SLOTS, 2, 2])
        affine2 = sb("affine2", [P, 1, 2, 2])
        bn_in = sb("bn_in", [P, 4, BN_COLS])
        bn_std = sb("bn_std", [P, BN_COLS])
        bn_scale = sb("bn_scale", [P, BN_COLS])
        bn_shift = sb("bn_shift", [P, BN_COLS])

        conv_ps = [ctx.enter_context(nc.psum_tensor(f"conv_ps{b}", [P, 512], F32)) for b in range(BANKS)]
        gram_ps = [ctx.enter_context(nc.psum_tensor(f"gram_ps{s}", [P, 512], F32)) for s in range(2)]
        corner_ps = ctx.enter_context(nc.psum_tensor("corner_ps", [P, 512], F32))
        stat_ps = ctx.enter_context(nc.psum_tensor("stat_ps", [P, 512], F32))

        dist0 = const[:, 0:S]
        dist1 = const[0:S1, S:S + S1]
        group_mean = const[:, S + S1:CONSTS]
        staging = x_ring[:, 2:SLOTS].rearrange("p a s j n -> p (a s j n)")
        w_raw = (scratch[:, :, :, :].rearrange("p s j n -> p (s j n)")[:, 0:W_EARLY], staging[:, 0:W_ALL - W_EARLY])
        eye_raw = staging[:, W_ALL - W_EARLY:W_ALL - W_EARLY + P]
        w_parts = (w_hi, w_lo)
        w1 = [w[:, 0:W1].rearrange("p (j o) -> p j o", j=CJ) for w in w_parts]
        w2 = [w[:, W_EARLY:W_EARLY + W2].rearrange("p (k a o) -> p k a o", k=MC, a=TAPS) for w in w_parts]
        w3 = [[w[:, at:at + C].rearrange("p (j o) -> p j o", j=CJ) for at in (W1, W_EARLY + W2)] for w in w_parts]
        w_cols = (slice(0, W_EARLY), slice(W_EARLY, W_ALL))
        fb = (fb_hi, fb_lo)
        h1 = (h1_hi, h1_lo)
        h2 = (h2_hi, h2_lo)
        PRODUCTS = ((0, 0), (0, 1), (1, 0))

        x_loaded = [sem(f"x_loaded{i}") for i in range(SLOTS)]
        stored = [[sem(f"stored{h}_{i}") for i in range(SLOTS)] for h in range(2)]
        weights_loaded = [sem(f"weights_loaded{i}") for i in range(2)]
        eye_done = sem("eye_done")
        const_loaded = sem("const_loaded")
        eye_loaded = sem("eye_loaded")
        bn_loaded = sem("bn_loaded")
        fills_done = sem("fills_done")
        w_hi_done = sem("w_hi_done")
        w_lo_done = sem("w_lo_done")
        bn_std_done = sem("bn_std_done")
        bn_chain = sem("bn_chain")
        pieces_done = [sem(f"pieces_done{n}") for n in range(2)]
        moments_chain = [sem(f"moments_chain{n}") for n in range(2)]
        moments_done = [sem(f"moments_done{n}") for n in range(2)]
        group_summed = [sem(f"group_summed{n}") for n in range(2)]
        var_chain = [sem(f"var_chain{n}") for n in range(2)]
        var_done = [sem(f"var_done{n}") for n in range(2)]
        std_done = [sem(f"std_done{n}") for n in range(2)]
        scale_chain = [sem(f"scale_chain{n}") for n in range(2)]
        affine_done = [sem(f"affine_done{n}") for n in range(2)]
        f1_full = sem("f1_full")
        f1_hi = sem("f1_hi")
        f1_lo = sem("f1_lo")
        gram_done = sem("gram_done")
        diag_done = sem("diag_done")
        rows_added = sem("rows_added")
        half_copied = sem("half_copied")
        clamp_chain = sem("clamp_chain")
        clamped = sem("clamped")
        rooted = sem("rooted")
        damped = sem("damped")
        sums_done = sem("sums_done")
        diag_chain = sem("diag_chain")
        m_chain = sem("m_chain")
        m_split = sem("m_split")
        m_spread = sem("m_spread")
        m_done = sem("m_done")
        f1_again = sem("f1_again")
        m_f1 = sem("m_f1")
        x1_done = sem("x1_done")
        f2_full = sem("f2_full")
        f2_hi = sem("f2_hi")
        f2_lo = sem("f2_lo")
        f2_added = sem("f2_added")
        u_done = sem("u_done")
        filled = [sem(f"filled{b}") for b in range(BANKS)]
        squared = [sem(f"squared{b}") for b in range(BANKS)]
        h_affine = [sem(f"h{n}_affine") for n in (1, 2)]
        h_hi = [sem(f"h{n}_hi") for n in (1, 2)]
        h_lo = [sem(f"h{n}_lo") for n in (1, 2)]
        added = [sem(f"added{i}") for i in range(ZB)]

        def valid(j):
            return not isinstance(j, int) or 0 <= j < pairs

        def after(eng, s, value):
            if not isinstance(value, int) or value > 0:
                eng.wait_ge(s, value)

        def steps(eng, step):
            def one(q, k):
                step(SLOTS * q + k, lambda o: (k + o) % SLOTS, lambda o: q + (k + o) // SLOTS)

            for k in range(1, SLOTS):
                one(-1, k)
            whole = pairs // SLOTS - 1
            if whole > 0:
                with eng.Fori(0, whole) as q:
                    for k in range(SLOTS):
                        one(q, k)
            for k in range(SLOTS):
                one(whole, k)

        block = ctx.enter_context(nc.Block())

        @block.sync
        def _(sp):
            def load(pair, slot, half):
                sp.dma_start(x_ring[:, slot, :, HALVES[half]].rearrange("p s j n -> p s (j n)"),
                             pair[:, :, HALVES[half].start * S:HALVES[half].stop * S]).then_inc(x_loaded[slot], 16)

            for half in range(2):
                load(x_pairs[0], 0, half)
            sp.dma_start(bn_in[:, :, :], bn).then_inc(bn_loaded, 16)
            sp.dma_start(const[:, :], consts).then_inc(const_loaded, 16)
            sp.dma_start(eye_raw, identity).then_inc(eye_loaded, 16)
            sp.dma_start(w_raw[0], weights[:, 0:W_EARLY]).then_inc(weights_loaded[0], 16)
            for half in range(2):
                load(x_pairs[1], 1, half)
            sp.dma_start(w_raw[1], weights[:, W_EARLY:]).then_inc(weights_loaded[1], 16)
            sp.wait_ge(eye_done, 1)
            sp.wait_ge(w_lo_done, 2)
            for half in range(2):
                load(x_pairs[2], 2, half)

            def step(t, slot, visit):
                if isinstance(t, int) and t < 0:
                    return
                if valid(t + 3):
                    for half in range(2):
                        after(sp, stored[half][slot(3)], 16 * visit(3))
                        load(x_pairs[bass.ds(t + 3, 1)].rearrange("q p s n -> (q p) s n"), slot(3), half)
                for half in range(2):
                    for i in range(ZB):
                        sp.wait_ge(added[i], 2 * t + 1 + half)
                    sp.dma_start(out_pairs[bass.ds(t, 1)].rearrange("q p s n -> (q p) s n")[
                                     :, :, HALVES[half].start * S:HALVES[half].stop * S],
                                 x_ring[:, slot(0), :, HALVES[half]].rearrange("p s j n -> p s (j n)")
                                 ).then_inc(stored[half][slot(0)], 16)

            steps(sp, step)
            for half in range(2):
                for i in range(SLOTS):
                    sp.wait_ge(stored[half][i], 16 * (pairs // SLOTS))

        @block.gpsimd
        def _(pool):
            nc.gpsimd.memset(ones[:, :], 1.0)
            nc.gpsimd.memset(h1_hi[:, :, :, :, :].bitcast(F32), 0.0)
            nc.gpsimd.memset(h1_lo[:, :, :, :, :].bitcast(F32), 0.0).then_inc(fills_done, 1)
            for i in range(2):
                pool.wait_ge(w_hi_done, i + 1)
                nc.gpsimd.tensor_tensor(w_lo[:, w_cols[i]], w_raw[i], w_hi[:, w_cols[i]].bitcast(F32), ALU.subtract
                                        ).then_inc(w_lo_done, 1)
            pool.wait_ge(bn_chain, 9)

            def step(t, slot, visit):
                b = t + 1
                if not valid(b):
                    return
                for s in range(2):
                    n = 2 * b + s
                    at = x_ring[:, slot(1), s]
                    pool.wait_ge(f1_again, n + 1)
                    pool.wait_ge(m_done, n + 1)
                    nc.gpsimd.tensor_tensor(scratch[:, s], scratch[:, s],
                                            m_all[:, s].unsqueeze(1).to_broadcast([P, CJ, S]),
                                            ALU.mult).then_inc(m_f1, 1)
                    pool.wait_ge(m_f1, n + 1)
                    nc.gpsimd.tensor_tensor(at, scratch[:, s], at, ALU.add).then_inc(x1_done, 1)
                for s in range(2):
                    n = 2 * b + s
                    at = x_ring[:, slot(1), s]
                    pool.wait_ge(f2_full, n + 1)
                    pool.wait_ge(pieces_done[1], n + 1)
                    nc.gpsimd.tensor_tensor(at, at, f_full[:, s], ALU.add).then_inc(f2_added, 1)
                    pool.wait_ge(f2_added, n + 1)
                    nc.gpsimd.tensor_tensor(at, at, bn_shift[:, BN_LAST:].unsqueeze(2).to_broadcast([P, CJ, S]),
                                            ALU.add).then_inc(u_done, 1)

            steps(pool, step)

        @block.scalar
        def _(act):
            act.wait_ge(bn_loaded, 16)
            act.wait_ge(bn_chain, 1)
            nc.scalar.activation(bn_std[:, :], bn_in[:, 3, :], ACT.Sqrt).then_inc(bn_std_done, 1)

            def w_hi_of(i):
                act.wait_ge(weights_loaded[i], 16)
                nc.scalar.activation(w_hi[:, w_cols[i]], w_raw[i], ACT.Copy).then_inc(w_hi_done, 1)


            def root_var(n, j):
                act.wait_ge(var_done[n], j + 1)
                nc.scalar.activation(std[n][:, :], var[n][:, :], ACT.Sqrt).then_inc(std_done[n], 1)

            def f1_of(j, s, slot):
                act.wait_ge(affine_done[0], j + 1)
                after(act, f2_added, 2 * j + s - 3)
                nc.scalar.activation(f_full[:, s], x_ring[:, slot, s], ACT.Identity,
                                     bias=affine1[:, slot, s, 1:2], scale=affine1[:, slot, s, 0:1]
                                     ).then_inc(f1_full, 1)

            def f1_again_of(j, s, slot):
                if isinstance(j, int) and j == 0:
                    act.wait_ge(w_lo_done, 1)
                after(act, x1_done, 2 * j + s - 1)
                nc.scalar.activation(scratch[:, s], x_ring[:, slot, s], ACT.Identity,
                                     bias=affine1[:, slot, s, 1:2], scale=affine1[:, slot, s, 0:1]
                                     ).then_inc(f1_again, 1)

            def f1_hi_of(j, s):
                act.wait_ge(f1_full, 2 * j + s + 1)
                after(act, gram_done, 2 * j + s)
                nc.scalar.activation(fa[:, :, 0], f_full[:, s], ACT.Copy).then_inc(f1_hi, 1)

            def f2_of(j, s, slot):
                act.wait_ge(affine_done[1], j + 1)
                if valid(j + 1):
                    act.wait_ge(f1_lo, 2 * j + s + 3)
                nc.scalar.activation(f_full[:, s], x_ring[:, slot, s], ACT.Identity,
                                     bias=affine2[:, 0, s, 1:2], scale=affine2[:, 0, s, 0:1]
                                     ).then_inc(f2_full, 1)

            def f2_hi_of(j, s):
                act.wait_ge(f2_full, 2 * j + s + 1)
                after(act, filled[1], 3 * j - 2)
                nc.scalar.activation(fb_hi[:, s], f_full[:, s], ACT.Copy).then_inc(f2_hi, 1)

            def copy_half(j, s):
                act.wait_ge(diag_chain, 2 * (2 * j + s) + 1)
                nc.scalar.activation(d0[:, s], gram_ps[s][:, S:2 * S], ACT.Copy, scale=2.0)
                nc.scalar.activation(d1[:, s], corner_ps[0:S1, S1:2 * S1], ACT.Copy, scale=2.0
                                     ).then_inc(half_copied, 1)

            def root_d(j, s):
                act.wait_ge(clamped, 2 * j + s + 1)
                nc.scalar.activation(d0[:, s], d0[:, s], ACT.Sqrt, bias=sq0[:, s:s + 1], scale=-1.0)
                nc.scalar.activation(d1[:, s], d1[:, s], ACT.Sqrt, bias=sq1[:, s:s + 1], scale=-1.0
                                     ).then_inc(rooted, 1)

            def m_of(j, s):
                act.wait_ge(m_spread, 2 * j + s + 1)
                after(act, m_f1, 2 * j + s - 1)
                nc.scalar.activation(m_all[:, s], gram_ps[s][:, 0:S], ACT.Copy).then_inc(m_done, 1)

            def square(t, layer, m):
                bank = 2 * layer + m
                if layer == 0:
                    act.wait_ge(added[m], 2 * t)
                act.wait_ge(filled[bank], 3 * t + 1)
                if layer == 0:
                    to = z[:, m].rearrange("p (n s) -> p s n", s=2)
                    y = conv_ps[bank][:, 0:2 * S].rearrange("p (s n) -> p s n", s=2)
                else:
                    to, y = z[:, m], conv_ps[bank][:, 0:2 * S]
                nc.scalar.activation(to, y, ACT.Square, bias=1.0).then_inc(squared[bank], 1)

            def h_hi_of(t, layer, m):
                act.wait_ge(h_affine[layer], 2 * t + m + 1)
                if layer == 0:
                    nc.scalar.activation(h1_hi[:, m, 1:1 + SIDE, 1:1 + SIDE, :],
                                         z[:, m].rearrange("p (h w s) -> p h w s", s=2, h=SIDE), ACT.Copy
                                         ).then_inc(h_hi[0], 1)
                else:
                    nc.scalar.activation(h2_hi[:, m], z[:, m], ACT.Copy).then_inc(h_hi[1], 1)

            def square_last(t, j):
                bank, buf = j % BANKS, (j + MC) % ZB
                act.wait_ge(filled[bank], 3 * t + 2 + j // BANKS)
                act.wait_ge(added[buf], 2 * t + j // ZB)
                nc.scalar.activation(z[:, buf].rearrange("p (s n) -> p s n", s=2),
                                     conv_ps[bank][:, 0:2 * S].rearrange("p (n s) -> p s n", s=2),
                                     ACT.Square, bias=1.0).then_inc(squared[bank], 1)

            def step(t, slot, visit):
                a, b, c, e = valid(t + 2), valid(t + 1), valid(t), valid(t + 3)
                if isinstance(t, int) and t == -3:
                    w_hi_of(0)
                if a:
                    f1_of(t + 2, 0, slot(2))
                    f1_hi_of(t + 2, 0)
                if c:
                    square(t, 0, 0)
                if b:
                    m_of(t + 1, 1)
                if c:
                    h_hi_of(t, 0, 0)
                if a:
                    f1_of(t + 2, 1, slot(2))
                if c:
                    square(t, 0, 1)
                    h_hi_of(t, 0, 1)
                if a:
                    f1_hi_of(t + 2, 1)
                    copy_half(t + 2, 0)
                    f1_again_of(t + 2, 0, slot(2))
                    f1_again_of(t + 2, 1, slot(2))
                    root_d(t + 2, 0)
                if b:
                    root_var(1, t + 1)
                if c:
                    square(t, 1, 0)
                    h_hi_of(t, 1, 0)
                if b:
                    f2_of(t + 1, 0, slot(1))
                    f2_hi_of(t + 1, 0)
                    f2_of(t + 1, 1, slot(1))
                    f2_hi_of(t + 1, 1)
                if c:
                    square(t, 1, 1)
                    h_hi_of(t, 1, 1)
                if a:
                    m_of(t + 2, 0)
                    copy_half(t + 2, 1)
                if c:
                    for j in range(0, 4):
                        square_last(t, j)
                if a:
                    root_d(t + 2, 1)
                if c:
                    for j in range(4, 7):
                        square_last(t, j)
                if e:
                    root_var(0, t + 3)
                if c:
                    square_last(t, 7)
                if isinstance(t, int) and t == -3:
                    w_hi_of(1)

            steps(act, step)

        @block.vector
        def _(dve):
            dve.wait_ge(bn_loaded, 16)
            nc.vector.tensor_scalar_add(bn_in[:, 3, :], bn_in[:, 3, :], BN_EPS).then_inc(bn_chain, 1)
            dve.wait_ge(bn_std_done, 1)
            nc.vector.reciprocal(bn_std[:, :], bn_std[:, :]).then_inc(bn_chain, 1)
            dve.wait_ge(bn_chain, 2)
            nc.vector.tensor_tensor(bn_scale[:, :], bn_in[:, 3, :], bn_std[:, :], ALU.mult).then_inc(bn_chain, 1)
            dve.wait_ge(bn_chain, 3)
            nc.vector.tensor_tensor(bn_scale[:, :], bn_scale[:, :], bn_std[:, :], ALU.mult).then_inc(bn_chain, 1)
            dve.wait_ge(bn_chain, 4)
            nc.vector.tensor_scalar(bn_scale[:, :], bn_scale[:, :], -0.5, 1.5, ALU.mult, ALU.add).then_inc(bn_chain, 1)
            dve.wait_ge(bn_chain, 5)
            nc.vector.tensor_tensor(bn_std[:, :], bn_scale[:, :], bn_std[:, :], ALU.mult).then_inc(bn_chain, 1)
            dve.wait_ge(bn_chain, 6)
            nc.vector.tensor_tensor(bn_scale[:, :], bn_in[:, 0, :], bn_std[:, :], ALU.mult).then_inc(bn_chain, 1)
            dve.wait_ge(bn_chain, 7)
            nc.vector.tensor_tensor(bn_shift[:, :], bn_in[:, 2, :], bn_scale[:, :], ALU.mult).then_inc(bn_chain, 1)
            dve.wait_ge(bn_chain, 8)
            nc.vector.tensor_tensor(bn_shift[:, :], bn_in[:, 1, :], bn_shift[:, :], ALU.subtract).then_inc(bn_chain, 1)
            dve.wait_ge(bn_chain, 9)
            dve.wait_ge(eye_loaded, 16)
            nc.vector.tensor_copy(eye[:, :], eye_raw).then_inc(eye_done, 1)
            dve.wait_ge(const_loaded, 16)

            def stat_pieces(n, j, s, slot):
                row = x_ring[:, slot, s].rearrange("p (a j) n -> p a (j n)", a=STAT_PIECES)
                for a in range(STAT_PIECES):
                    last = nc.vector.bn_stats(pieces[n][:, s, a, :], row[:, a])
                last.then_inc(pieces_done[n], 1)

            def moments_of(n, j):
                dve.wait_ge(pieces_done[n], 2 * j + 2)
                nc.vector.tensor_copy(mean_sq[n][:, 0:1], pieces[n][:, 1, 0, 0:1])
                for s in range(2):
                    last = nc.vector.bn_aggr(moments[n][:, s, :], pieces[n][:, s].rearrange("p a e -> p (a e)"))
                last.then_inc(moments_chain[n], 1)
                dve.wait_ge(moments_chain[n], 2 * j + 1)
                nc.vector.tensor_tensor(mean_sq[n][:, :], moments[n][:, :, 0], moments[n][:, :, 0], ALU.mult
                                        ).then_inc(moments_chain[n], 1)
                dve.wait_ge(moments_chain[n], 2 * j + 2)
                nc.vector.tensor_tensor(moments[n][:, :, 1], moments[n][:, :, 1], mean_sq[n][:, :], ALU.add
                                        ).then_inc(moments_done[n], 1)

            def group_var(n, j):
                dve.wait_ge(group_summed[n], j + 1)
                nc.vector.tensor_copy(group[n][:, :, :].rearrange("p s e -> p (s e)"), stat_ps[:, 4 * n:4 * n + 4]
                                      ).then_inc(var_chain[n], 1)
                dve.wait_ge(var_chain[n], 3 * j + 1)
                nc.vector.tensor_tensor(mean_sq[n][:, :], group[n][:, :, 0], group[n][:, :, 0], ALU.mult
                                        ).then_inc(var_chain[n], 1)
                dve.wait_ge(var_chain[n], 3 * j + 2)
                nc.vector.tensor_tensor(var[n][:, :], group[n][:, :, 1], mean_sq[n][:, :], ALU.subtract
                                        ).then_inc(var_chain[n], 1)
                dve.wait_ge(var_chain[n], 3 * j + 3)
                nc.vector.tensor_scalar(var[n][:, :], var[n][:, :], 0.0, GN_EPS, ALU.max, ALU.add
                                        ).then_inc(var_done[n], 1)

            def affine_of(n, j, to):
                dve.wait_ge(std_done[n], j + 1)
                nc.vector.reciprocal(rec[n][:, :], std[n][:, :]).then_inc(scale_chain[n], 1)
                dve.wait_ge(scale_chain[n], 5 * j + 1)
                nc.vector.tensor_tensor(mean_sq[n][:, :], var[n][:, :], rec[n][:, :], ALU.mult
                                        ).then_inc(scale_chain[n], 1)
                dve.wait_ge(scale_chain[n], 5 * j + 2)
                nc.vector.tensor_tensor(mean_sq[n][:, :], mean_sq[n][:, :], rec[n][:, :], ALU.mult
                                        ).then_inc(scale_chain[n], 1)
                dve.wait_ge(scale_chain[n], 5 * j + 3)
                nc.vector.tensor_scalar(mean_sq[n][:, :], mean_sq[n][:, :], -0.5, 1.5, ALU.mult, ALU.add
                                        ).then_inc(scale_chain[n], 1)
                dve.wait_ge(scale_chain[n], 5 * j + 4)
                nc.vector.tensor_tensor(to[:, :, 0], mean_sq[n][:, :], rec[n][:, :], ALU.mult
                                        ).then_inc(scale_chain[n], 1)
                dve.wait_ge(scale_chain[n], 5 * j + 5)
                nc.vector.scalar_tensor_tensor(to[:, :, 1], group[n][:, :, 0], -1.0, to[:, :, 0],
                                               ALU.mult, ALU.mult).then_inc(affine_done[n], 1)

            def f1_lo_of(j, s):
                dve.wait_ge(f1_hi, 2 * j + s + 1)
                nc.vector.tensor_tensor(fa[:, :, 1], f_full[:, s], fa[:, :, 0].bitcast(F32), ALU.subtract
                                        ).then_inc(f1_lo, 1)

            def f2_lo_of(j, s):
                dve.wait_ge(f2_hi, 2 * j + s + 1)
                nc.vector.tensor_tensor(fb_lo[:, s], f_full[:, s], fb_hi[:, s].bitcast(F32), ALU.subtract
                                        ).then_inc(f2_lo, 1)

            def diag_of(j, s):
                n = 2 * j + s
                dve.wait_ge(gram_done, n + 1)
                nc.vector.tensor_tensor_reduce(
                    out=d0[:, :, 0:P], in0=gram_ps[s][:, 0:2 * S].rearrange("p (a n) -> p a n", a=2)[:, :, 0:P],
                    in1=eye[:, :].bitcast(F32).unsqueeze(1).to_broadcast([P, 2, P]),
                    scale=1.0, scalar=0.0, op0=ALU.mult, op1=ALU.add, accum_out=sq0[:, s:s + 1])
                nc.vector.tensor_tensor_reduce(
                    out=d1[:, :, :], in0=corner_ps[0:S1, 0:2 * S1].rearrange("p (a n) -> p a n", a=2),
                    in1=eye[0:S1, 0:S1].bitcast(F32).unsqueeze(1).to_broadcast([S1, 2, S1]),
                    scale=1.0, scalar=0.0, op0=ALU.mult, op1=ALU.add, accum_out=sq1[:, s:s + 1]
                    ).then_inc(diag_chain, 1)
                dve.wait_ge(diag_chain, 2 * n + 1)
                nc.vector.tensor_scalar(pixel0[:, s, 0:1], sq0[:, s:s + 1], -0.5, None, ALU.mult)
                nc.vector.tensor_scalar(pixel1[:, s, 0:1], sq1[:, s:s + 1], -0.5, None, ALU.mult
                                        ).then_inc(diag_chain, 1)
                dve.wait_ge(diag_chain, 2 * n + 2)
                nc.vector.scalar_tensor_tensor(pixel0[:, s, 1:2], sq0[:, s:s + 1], -0.5,
                                               pixel0[:, s, 0:1].bitcast(F32), ALU.mult, ALU.subtract)
                nc.vector.scalar_tensor_tensor(pixel1[:, s, 1:2], sq1[:, s:s + 1], -0.5,
                                               pixel1[:, s, 0:1].bitcast(F32), ALU.mult, ALU.subtract
                                               ).then_inc(diag_done, 1)

            def clamp(j, s):
                n = 2 * j + s
                dve.wait_ge(half_copied, n + 1)
                dve.wait_ge(rows_added, n + 1)
                nc.vector.scalar_tensor_tensor(d0[:, s], gram_ps[s][:, 0:S], 2.0, d0[:, s], ALU.mult, ALU.add)
                nc.vector.scalar_tensor_tensor(d1[:, s], corner_ps[0:S1, 0:S1], 2.0, d1[:, s], ALU.mult, ALU.add
                                               ).then_inc(clamp_chain, 1)
                dve.wait_ge(clamp_chain, n + 1)
                nc.vector.tensor_scalar(d0[:, s], d0[:, s], sq0[:, s:s + 1], None, ALU.min)
                nc.vector.tensor_scalar(d1[:, s], d1[:, s], sq1[:, s:s + 1], None, ALU.min
                                        ).then_inc(clamped, 1)

            def damp(j, s):
                dve.wait_ge(rooted, 2 * j + s + 1)
                nc.vector.tensor_tensor_reduce(out=d0[:, s], in0=d0[:, s], in1=dist0, scale=1.0, scalar=0.0,
                                               op0=ALU.mult, op1=ALU.add, accum_out=sum0[:, s:s + 1])
                nc.vector.tensor_tensor(d1[:, s], d1[:, s], dist1, ALU.mult).then_inc(damped, 1)

            def new_m(j, s):
                n = 2 * j + s
                dve.wait_ge(sums_done, n + 1)
                nc.vector.tensor_copy(sum1[:, s:s + 1], gram_ps[s][0:S1, S:S + 1])
                nc.vector.reciprocal(rec0[:, s:s + 1], sum0[:, s:s + 1]).then_inc(m_chain, 1)
                dve.wait_ge(m_chain, 3 * n + 1)
                nc.vector.reciprocal(rec1[:, s:s + 1], sum1[:, s:s + 1]).then_inc(m_chain, 1)
                dve.wait_ge(m_chain, 3 * n + 2)
                for to in (m0[:, s:s + 1], pixel0[:, s, 0:1]):
                    nc.vector.tensor_scalar(to, sum0[:, s:s + 1], 1.0 / S, rec0[:, s:s + 1], ALU.mult, ALU.mult)
                for to in (m1[:, s:s + 1], pixel1[:, s, 0:1]):
                    last = nc.vector.tensor_scalar(to, sum1[:, s:s + 1], 1.0 / S, rec1[:, s:s + 1],
                                                   ALU.mult, ALU.mult)
                last.then_inc(m_chain, 1)
                dve.wait_ge(m_chain, 3 * n + 3)
                nc.vector.tensor_tensor(pixel0[:, s, 1:2], m0[:, s:s + 1], pixel0[:, s, 0:1].bitcast(F32),
                                        ALU.subtract)
                nc.vector.tensor_tensor(pixel1[:, s, 1:2], m1[:, s:s + 1], pixel1[:, s, 0:1].bitcast(F32),
                                        ALU.subtract).then_inc(m_split, 1)

            def h_affine_of(t, layer, m):
                col = MC * layer + m
                dve.wait_ge(squared[2 * layer + m], 3 * t + 1)
                nc.vector.tensor_scalar(z[:, m], z[:, m], bn_scale[:, col:col + 1], bn_shift[:, col:col + 1],
                                        ALU.mult, ALU.add).then_inc(h_affine[layer], 1)

            def h_lo_of(t, layer, m):
                dve.wait_ge(h_hi[layer], 2 * t + m + 1)
                if layer == 0:
                    inner = (slice(None), m, slice(1, 1 + SIDE), slice(1, 1 + SIDE), slice(None))
                    nc.vector.tensor_tensor(h1_lo[inner], z[:, m].rearrange("p (h w s) -> p h w s", s=2, h=SIDE),
                                            h1_hi[inner].bitcast(F32), ALU.subtract).then_inc(h_lo[0], 1)
                else:
                    nc.vector.tensor_tensor(h2_lo[:, m], z[:, m], h2_hi[:, m].bitcast(F32), ALU.subtract
                                            ).then_inc(h_lo[1], 1)

            def add_last(t, j, slot):
                if j == 0:
                    dve.wait_ge(u_done, 2 * t + 2)
                dve.wait_ge(squared[j % BANKS], 3 * t + 2 + j // BANKS)
                at, buf = x_ring[:, slot, :, j], (j + MC) % ZB
                nc.vector.scalar_tensor_tensor(at, z[:, buf].rearrange("p (s n) -> p s n", s=2),
                                               bn_scale[:, BN_LAST + j:BN_LAST + j + 1], at,
                                               ALU.mult, ALU.add).then_inc(added[buf], 1)

            def step(t, slot, visit):
                a, b, c, e = valid(t + 2), valid(t + 1), valid(t), valid(t + 3)
                if b:
                    new_m(t + 1, 1)
                if a:
                    f1_lo_of(t + 2, 0)
                if c:
                    h_affine_of(t, 0, 0)
                    h_lo_of(t, 0, 0)
                if b:
                    dve.wait_ge(x1_done, 2 * (t + 1) + 1)
                    stat_pieces(1, t + 1, 0, slot(1))
                if c:
                    h_affine_of(t, 0, 1)
                    h_lo_of(t, 0, 1)
                if a:
                    diag_of(t + 2, 0)
                if b:
                    dve.wait_ge(x1_done, 2 * (t + 1) + 2)
                    stat_pieces(1, t + 1, 1, slot(1))
                    moments_of(1, t + 1)
                if a:
                    f1_lo_of(t + 2, 1)
                    clamp(t + 2, 0)
                if b:
                    group_var(1, t + 1)
                    affine_of(1, t + 1, affine2[:, 0])
                if c:
                    h_affine_of(t, 1, 0)
                if a:
                    damp(t + 2, 0)
                if e:
                    dve.wait_ge(x_loaded[slot(3)], 32 * visit(3) + 32)
                    stat_pieces(0, t + 3, 0, slot(3))
                if c:
                    h_lo_of(t, 1, 0)
                if a:
                    new_m(t + 2, 0)
                if b:
                    f2_lo_of(t + 1, 0)
                if e:
                    stat_pieces(0, t + 3, 1, slot(3))
                    moments_of(0, t + 3)
                if c:
                    h_affine_of(t, 1, 1)
                    h_lo_of(t, 1, 1)
                if a:
                    diag_of(t + 2, 1)
                if c:
                    add_last(t, 0, slot(0))
                if c:
                    add_last(t, 1, slot(0))
                if a:
                    clamp(t + 2, 1)
                if c:
                    add_last(t, 2, slot(0))
                if b:
                    f2_lo_of(t + 1, 1)
                if c:
                    add_last(t, 3, slot(0))
                if a:
                    damp(t + 2, 1)
                if c:
                    add_last(t, 4, slot(0))
                if e:
                    group_var(0, t + 3)
                if c:
                    add_last(t, 5, slot(0))
                if c:
                    add_last(t, 6, slot(0))
                if c:
                    add_last(t, 7, slot(0))
                if e:
                    affine_of(0, t + 3, affine1[:, slot(3)])

            steps(dve, step)

        @block.tensor
        def _(pe):
            pe.wait_ge(const_loaded, 16)
            pe.wait_ge(eye_done, 1)

            def gram(j, s):
                n = 2 * j + s
                after(pe, m_done, n - 1)
                pe.wait_ge(f1_lo, n + 1)
                for c in range(CJ):
                    nc.tensor.matmul(gram_ps[s][:, 0:2 * S], fa[:, c, 0, 0:P], fa[:, c].rearrange("p a n -> p (a n)"),
                                     start=c == 0, stop=False, skip_group_check=True)
                    nc.tensor.matmul(gram_ps[s][:, 0:S], fa[:, c, 1, 0:P], fa[:, c, 0],
                                     start=False, stop=False, skip_group_check=True)
                after(pe, clamped, n)
                for c in range(CJ):
                    nc.tensor.matmul(corner_ps[0:S1, 0:2 * S1], fa[:, c, 0, P:S], fa[:, c, :, P:S],
                                     start=c == 0, stop=False, skip_group_check=True)
                    last = nc.tensor.matmul(corner_ps[0:S1, 0:S1], fa[:, c, 1, P:S], fa[:, c, 0, P:S],
                                            start=False, stop=False, skip_group_check=True)
                last.then_inc(gram_done, 1)

            def spread_pixels(s, other_rows, start):
                for i in range(2):
                    of0 = pixel0[:, s, i:i + 1].to_broadcast([P, P])
                    of1 = pixel1[:, s, i:i + 1].to_broadcast([S1, P])
                    nc.tensor.matmul(gram_ps[s][:, 0:P], of0, eye[:, :], start=start and i == 0, stop=False,
                                     skip_group_check=True)
                    last = nc.tensor.matmul(gram_ps[s][:, P:S], of1, eye[0:S1, 0:S1], start=False, stop=i == 1,
                                            skip_group_check=True)
                    if other_rows:
                        last = nc.tensor.matmul(corner_ps[0:S1, 0:S1], pixel1[:, s, i:i + 1].to_broadcast([S1, S1]),
                                                eye[0:S1, 0:S1], start=False, stop=i == 1, skip_group_check=True)
                return last

            def add_rows(j, s):
                pe.wait_ge(diag_done, 2 * j + s + 1)
                pe.wait_ge(half_copied, 2 * j + s + 1)
                spread_pixels(s, other_rows=True, start=False).then_inc(rows_added, 1)

            def sum_rows(j, s):
                pe.wait_ge(damped, 2 * j + s + 1)
                nc.tensor.matmul(gram_ps[s][0:S1, S:S + 1], d0[:, s, P:S], ones[:, :], start=True, stop=False)
                nc.tensor.matmul(gram_ps[s][0:S1, S:S + 1], d1[:, s], ones[0:S1, :], start=False, stop=True
                                 ).then_inc(sums_done, 1)

            def spread_m(j, s):
                pe.wait_ge(m_split, 2 * j + s + 1)
                spread_pixels(s, other_rows=False, start=True).then_inc(m_spread, 1)

            def sum_group(n, j):
                pe.wait_ge(moments_done[n], j + 1)
                if n == 1 and valid(j + 1):
                    after(pe, var_chain[0], 3 * j + 4)
                if n == 0:
                    after(pe, var_chain[1], 3 * j - 5)
                nc.tensor.matmul(stat_ps[:, 4 * n:4 * n + 4], group_mean, moments[n][:, :, :].rearrange("p s e -> p (s e)"),
                                 start=True, stop=True).then_inc(group_summed[n], 1)

            def conv1(t, m):
                if isinstance(t, int) and t == 0 and m == 0:
                    pe.wait_ge(fills_done, 1)
                    pe.wait_ge(w_lo_done, 2)
                if m == 0:
                    pe.wait_ge(f2_lo, 2 * t + 2)
                pe.wait_ge(squared[m], 3 * t)
                for j in range(CJ):
                    for i, (w, f) in enumerate(PRODUCTS):
                        last = nc.tensor.matmul(conv_ps[m][:, 0:2 * S], w1[w][:, j, m * P:(m + 1) * P],
                                                fb[f][:, :, j], start=(j == 0 and i == 0),
                                                stop=(j == CJ - 1 and i == 2))
                last.then_inc(filled[m], 1)

            def conv2(t, m, k, taps=(1, 0, 2)):
                bank = 2 + m
                if k == 0:
                    pe.wait_ge(squared[bank], 3 * t)
                if m == 0 and 1 in taps:
                    pe.wait_ge(h_lo[0], 2 * t + k + 1)
                for dy in taps:
                    top, bottom = max(1 - dy, 0), SIDE - max(dy - 1, 0)
                    for dx in (1, 0, 2):
                        left, right = max(1 - dx, 0), SIDE - max(dx - 1, 0)
                        to = conv_ps[bank][:, 0:2 * S].rearrange("p (h w) -> p h w", h=SIDE)[
                            :, top:bottom, 2 * left:2 * right]
                        for i, (w, f) in enumerate(PRODUCTS):
                            last = nc.tensor.matmul(to, w2[w][:, k, 3 * dy + dx, m * P:(m + 1) * P],
                                                    h1[f][:, k, top + dy:bottom + dy, left + dx:right + dx, :]
                                                    .rearrange("p h w s -> p h (w s)"),
                                                    start=(k == 0 and dy == 1 and dx == 1 and i == 0),
                                                    stop=(k == MC - 1 and dy == 2 and dx == 2 and i == 2))
                if k == MC - 1 and 2 in taps:
                    last.then_inc(filled[bank], 1)

            def conv3(t, j):
                bank = j % BANKS
                if j == 0:
                    pe.wait_ge(h_lo[1], 2 * t + 2)
                pe.wait_ge(squared[bank], 3 * t + 1 + j // BANKS)
                for k in range(MC):
                    for i, (w, f) in enumerate(PRODUCTS):
                        last = nc.tensor.matmul(conv_ps[bank][:, 0:2 * S], w3[w][k][:, j], h2[f][:, k],
                                                start=(k == 0 and i == 0), stop=(k == MC - 1 and i == 2))
                last.then_inc(filled[bank], 1)

            def step(t):
                a, b, c, e = valid(t + 2), valid(t + 1), valid(t), valid(t + 3)
                if c:
                    conv1(t, 0)
                if b:
                    spread_m(t + 1, 1)
                if c:
                    conv1(t, 1)
                if a:
                    gram(t + 2, 0)
                if c:
                    conv2(t, 0, 0)
                if a:
                    add_rows(t + 2, 0)
                if c:
                    conv2(t, 0, 1, taps=[1])
                if b:
                    sum_group(1, t + 1)
                if c:
                    conv2(t, 0, 1, taps=[0, 2])
                    conv2(t, 1, 0)
                if a:
                    sum_rows(t + 2, 0)
                if c:
                    conv2(t, 1, 1)
                if a:
                    spread_m(t + 2, 0)
                    gram(t + 2, 1)
                if c:
                    for j in range(0, 2):
                        conv3(t, j)
                if a:
                    add_rows(t + 2, 1)
                if c:
                    for j in range(2, 6):
                        conv3(t, j)
                if e:
                    sum_group(0, t + 3)
                if c:
                    for j in range(6, 8):
                        conv3(t, j)
                if a:
                    sum_rows(t + 2, 1)

            for t in range(-3, 1):
                step(t)
            if pairs > 4:
                with pe.Fori(1, pairs - 3) as t:
                    step(t)
            for t in range(max(pairs - 3, 0), pairs):
                step(t)


def constants():
    import numpy as np

    at = np.stack(np.meshgrid(np.arange(SIDE), np.arange(SIDE), indexing="ij")).reshape(2, -1)
    d2 = ((at[:, :, None] - at[:, None, :]) ** 2).sum(0).astype(np.float32)
    dist = np.exp(-d2 / np.float32(2.0 * (0.15 * SIDE) ** 2)).astype(np.float32)
    table = np.zeros((P, CONSTS), np.float32)
    table[:, 0:S] = dist[0:P]
    table[0:S1, S:S + S1] = dist[P:, P:]
    p = np.arange(P) // GROUP_PARTS
    table[:, S + S1:] = (p[:, None] == p[None, :]) / np.float32(GROUP_PARTS)
    return table


def laid_out(inputs):
    import numpy as np

    a = {k: np.asarray(v) for k, v in inputs.items()}
    w1 = a["L1_conv_w1"].reshape(MID, P, CJ).transpose(1, 2, 0).reshape(P, W1)
    w2 = a["L1_conv_w2"].reshape(MID, MC, P, TAPS).transpose(2, 1, 3, 0).reshape(P, W2)
    w3 = a["L1_conv_w3"].reshape(P, CJ, MC, P).transpose(3, 2, 1, 0).reshape(P, MC, C)
    bn = []
    for what in "gbmv":
        cols = [a[f"L1_conv_{what}{i}"].reshape(MC, P).T for i in (1, 2)]
        bn.append(np.concatenate(cols + [a[f"L1_conv_{what}3"].reshape(P, CJ)], axis=1))
    return {
        "x": np.ascontiguousarray(a["x"]),
        "weights": np.ascontiguousarray(np.concatenate([w1, w3[:, 0], w2, w3[:, 1]], axis=1)),
        "bn": np.ascontiguousarray(np.stack(bn, axis=1)),
        "identity": np.eye(P, dtype=np.float32),
        "consts": constants(),
    }


def kernel(**inputs):
    import concourse.bacc as bacc
    from concourse.bass_utils import run_bass_kernel_spmd

    nc = bacc.Bacc("TRN2", target_bir_lowering=False, num_devices=1)
    arrays = laid_out(inputs)
    args = [nc.dram_tensor(n, v.shape, F32, kind="ExternalInput").ap() for n, v in arrays.items()]
    out = nc.dram_tensor("out", arrays["x"].shape, F32, kind="ExternalOutput").ap()
    build(nc, *args, out)
    r = run_bass_kernel_spmd(nc, [arrays], core_ids=[0])
    return r.results[0]["out"]
```

```python
from contextlib import ExitStack

import concourse.bass as bass
from concourse import mybir

F32 = mybir.dt.float32
F32R = mybir.dt.float32r
ALU = mybir.AluOpType
ACT = mybir.ActivationFunctionType

P = 128
SIDE = 14
S = SIDE * SIDE
C = 1024
CJ = C // P
MID = 256
MC = MID // P
ROW = CJ * S
S1 = S - P
TAPS = 9
SLOTS = 4
ZB = 4
BANKS = 4
GROUP_PARTS = 4
GN_EPS = 1e-5
BN_EPS = 1e-5
W1, W2, W3 = CJ * MID, MC * TAPS * MID, MC * C
W_EARLY = W1 + C
W_ALL = W1 + W2 + W3
W_MID = W_EARLY + 2 * ROW
BN_COLS = MC + MC + CJ
BN_LAST = 2 * MC
STAT_PIECES = 4
HALVES = (slice(0, CJ // 2), slice(CJ // 2, CJ))
CONSTS = S + S1 + P


def build(nc, x, weights, bn, identity, consts, out):
    pairs = x.shape[0] // 2
    x_pairs = x.rearrange("(q s) (p j) h w -> q p s (j h w)", s=2, j=CJ)
    out_pairs = out.rearrange("(q s) (p j) h w -> q p s (j h w)", s=2, j=CJ)

    with ExitStack() as ctx:
        def sb(name, shape, dt=F32):
            return ctx.enter_context(nc.sbuf_tensor(name, shape, dt))

        def sem(name):
            return ctx.enter_context(nc.semaphore(name))

        x_ring = sb("x_ring", [P, SLOTS, 2, CJ, S])
        f_full = sb("f_full", [P, 2, CJ, S])
        scratch = sb("scratch", [P, 2, CJ, S])
        fa = sb("fa", [P, CJ, 2, S], F32R)
        fb_hi = sb("fb_hi", [P, 2, CJ, S], F32R)
        fb_lo = sb("fb_lo", [P, 2, CJ, S], F32R)
        w_hi = sb("w_hi", [P, W_ALL], F32R)
        w_lo = sb("w_lo", [P, W_ALL], F32R)
        h_parts = [[sb(f"h{n}_{part}", [P, MC, 2 * S], F32R) for part in ("hi", "lo")] for n in (1, 2)]
        z = sb("z", [P, ZB, 2 * S])
        const = sb("const", [P, CONSTS])
        eye_once_twice = sb("eye_once_twice", [P, 2, P], F32R)
        ones = sb("ones", [P, 1])
        pixel0 = sb("pixel0", [P, 2, 2], F32R)
        pixel1 = sb("pixel1", [S1, 2, 2], F32R)
        m0 = sb("m0", [P, 2])
        m1 = sb("m1", [S1, 2])
        sq0 = sb("sq0", [P, 2])
        sq1 = sb("sq1", [S1, 2])
        hl0 = sb("hl0", [P, S], F32R)
        hl1 = sb("hl1", [S1, S], F32R)
        d0 = sb("d0", [P, 2, S])
        d1 = sb("d1", [S1, 2, S1])
        sum0 = sb("sum0", [P, 2])
        sum1 = sb("sum1", [S1, 2])
        rec0 = sb("rec0", [P, 2])
        rec1 = sb("rec1", [S1, 2])
        m_all = sb("m_all", [P, 2, S])
        pieces = [sb(f"pieces{n}", [P, 2, STAT_PIECES, 6]) for n in range(2)]
        moments = [sb(f"moments{n}", [P, 2, 2]) for n in range(2)]
        mean_sq = [sb(f"mean_sq{n}", [P, 2]) for n in range(2)]
        group = [sb(f"group{n}", [P, 2, 2]) for n in range(2)]
        var = [sb(f"var{n}", [P, 2]) for n in range(2)]
        std = [sb(f"std{n}", [P, 2]) for n in range(2)]
        rec = [sb(f"rec_std{n}", [P, 2]) for n in range(2)]
        affine1 = sb("affine1", [P, SLOTS, 2, 2])
        affine2 = sb("affine2", [P, 1, 2, 2])
        bn_in = sb("bn_in", [P, 4, BN_COLS])
        bn_std = sb("bn_std", [P, BN_COLS])
        bn_scale = sb("bn_scale", [P, BN_COLS])
        bn_shift = sb("bn_shift", [P, BN_COLS])

        conv_ps = [ctx.enter_context(nc.psum_tensor(f"conv_ps{b}", [P, 512], F32)) for b in range(BANKS)]
        gram_ps = [ctx.enter_context(nc.psum_tensor(f"gram_ps{s}", [P, 512], F32)) for s in range(2)]
        corner_ps = ctx.enter_context(nc.psum_tensor("corner_ps", [P, 512], F32))
        stat_ps = ctx.enter_context(nc.psum_tensor("stat_ps", [P, 512], F32))

        eye = eye_once_twice[:, 0]
        bn_row = bn_in[:, :, :].rearrange("p a b -> p (a b)")
        u_shift = bn_row[:, 0:2 * CJ].rearrange("p (s j) -> p s j", s=2)
        u_scale = bn_row[:, 2 * CJ:2 * CJ + 2]
        u_gate = bn_row[:, 2 * CJ + 2:2 * CJ + 4]
        dist0 = const[:, 0:S]
        dist1 = const[0:S1, S:S + S1]
        group_mean = const[:, S + S1:CONSTS]
        staging = x_ring[:, 2:SLOTS].rearrange("p a s j n -> p (a s j n)")
        w_raw = (scratch[:, :, :, :].rearrange("p s j n -> p (s j n)")[:, 0:W_EARLY],
                 staging[:, 0:W_MID - W_EARLY], staging[:, W_MID - W_EARLY:W_ALL - W_EARLY])
        eye_raw = staging[:, W_ALL - W_EARLY:W_ALL - W_EARLY + P]
        w_parts = (w_hi, w_lo)
        w1 = [w[:, 0:W1].rearrange("p (j o) -> p j o", j=CJ) for w in w_parts]
        w2 = [w[:, W_EARLY:W_EARLY + W2].rearrange("p (k a o) -> p k a o", k=MC, a=TAPS) for w in w_parts]
        w3 = [[w[:, at:at + C].rearrange("p (j o) -> p j o", j=CJ) for at in (W1, W_EARLY + W2)] for w in w_parts]
        w_cols = (slice(0, W_EARLY), slice(W_EARLY, W_MID), slice(W_MID, W_ALL))
        fb = (fb_hi, fb_lo)
        h1 = [h[:, :, :].rearrange("p k (y x) -> p k y x", y=SIDE) for h in h_parts[0]]
        h2 = h_parts[1]
        PRODUCTS = ((0, 0), (0, 1), (1, 0))

        x_loaded = [sem(f"x_loaded{i}") for i in range(SLOTS)]
        stored = [[sem(f"stored{h}_{i}") for i in range(SLOTS)] for h in range(2)]
        weights_loaded = [sem(f"weights_loaded{i}") for i in range(3)]
        eye_done = sem("eye_done")
        const_loaded = sem("const_loaded")
        eye_loaded = sem("eye_loaded")
        bn_loaded = sem("bn_loaded")
        ones_done = sem("ones_done")
        w_hi_done = sem("w_hi_done")
        w_lo_done = [sem(f"w_lo_done{i}") for i in range(3)]
        bn_std_done = sem("bn_std_done")
        bn_chain = sem("bn_chain")
        pieces_done = [sem(f"pieces_done{n}") for n in range(2)]
        moments_chain = [sem(f"moments_chain{n}") for n in range(2)]
        moments_done = [sem(f"moments_done{n}") for n in range(2)]
        group_summed = [sem(f"group_summed{n}") for n in range(2)]
        var_chain = [sem(f"var_chain{n}") for n in range(2)]
        var_done = [sem(f"var_done{n}") for n in range(2)]
        std_done = [sem(f"std_done{n}") for n in range(2)]
        scale_chain = [sem(f"scale_chain{n}") for n in range(2)]
        affine_done = [sem(f"affine_done{n}") for n in range(2)]
        f1_full = sem("f1_full")
        f1_hi = sem("f1_hi")
        f1_lo = sem("f1_lo")
        gram_done = sem("gram_done")
        diag_done = sem("diag_done")
        rows_added = sem("rows_added")
        hl_copied = sem("hl_copied")
        clamp_chain = sem("clamp_chain")
        clamped = sem("clamped")
        rooted = sem("rooted")
        damped = sem("damped")
        sums_done = sem("sums_done")
        diag_chain = sem("diag_chain")
        m_chain = sem("m_chain")
        m_split = sem("m_split")
        m_spread = sem("m_spread")
        m_done = sem("m_done")
        f1_again = sem("f1_again")
        m_f1 = sem("m_f1")
        x1_done = sem("x1_done")
        f2_full = sem("f2_full")
        f2_hi = sem("f2_hi")
        f2_lo = sem("f2_lo")
        u_terms = sem("u_terms")
        u_done = sem("u_done")
        filled = [sem(f"filled{b}") for b in range(BANKS)]
        squared = [sem(f"squared{b}") for b in range(BANKS)]
        h_affine = [sem(f"h{n}_affine") for n in (1, 2)]
        h_hi = [sem(f"h{n}_hi") for n in (1, 2)]
        h_lo = [sem(f"h{n}_lo") for n in (1, 2)]
        added = [sem(f"added{i}") for i in range(ZB)]

        def valid(j):
            return not isinstance(j, int) or 0 <= j < pairs

        def after(eng, s, value):
            if not isinstance(value, int) or value > 0:
                eng.wait_ge(s, value)

        def steps(eng, step):
            def one(q, k):
                step(SLOTS * q + k, lambda o: (k + o) % SLOTS, lambda o: q + (k + o) // SLOTS)

            whole = pairs // SLOTS - 1
            if whole > 0:
                with eng.Fori(0, whole) as q:
                    for k in range(SLOTS):
                        one(q, k)
            for k in range(SLOTS):
                one(whole, k)

        block = ctx.enter_context(nc.Block())

        @block.sync
        def _(sp):
            def load(pair, slot, half):
                sp.dma_start(x_ring[:, slot, :, HALVES[half]].rearrange("p s j n -> p s (j n)"),
                             pair[:, :, HALVES[half].start * S:HALVES[half].stop * S]).then_inc(x_loaded[slot], 16)

            for half in range(2):
                load(x_pairs[0], 0, half)
            sp.dma_start(bn_in[:, :, :], bn).then_inc(bn_loaded, 16)
            sp.dma_start(const[:, :], consts).then_inc(const_loaded, 16)
            sp.dma_start(eye_raw, identity).then_inc(eye_loaded, 16)
            sp.dma_start(w_raw[0], weights[:, w_cols[0]]).then_inc(weights_loaded[0], 16)
            for half in range(2):
                load(x_pairs[1], 1, half)
            for i in (1, 2):
                sp.dma_start(w_raw[i], weights[:, w_cols[i]]).then_inc(weights_loaded[i], 16)
            sp.wait_ge(w_lo_done[1], 1)
            for half in range(2):
                load(x_pairs[2], 2, half)
            sp.wait_ge(eye_done, 1)
            sp.wait_ge(w_lo_done[2], 1)

            def step(t, slot, visit):
                if valid(t + 3):
                    for half in range(2):
                        after(sp, stored[half][slot(3)], 16 * visit(3))
                        load(x_pairs[bass.ds(t + 3, 1)].rearrange("q p s n -> (q p) s n"), slot(3), half)
                for half in range(2):
                    for i in range(ZB):
                        sp.wait_ge(added[i], 2 * t + 1 + half)
                    sp.dma_start(out_pairs[bass.ds(t, 1)].rearrange("q p s n -> (q p) s n")[
                                     :, :, HALVES[half].start * S:HALVES[half].stop * S],
                                 x_ring[:, slot(0), :, HALVES[half]].rearrange("p s j n -> p s (j n)")
                                 ).then_inc(stored[half][slot(0)], 16)

            steps(sp, step)
            for half in range(2):
                for i in range(SLOTS):
                    sp.wait_ge(stored[half][i], 16 * (pairs // SLOTS))

        @block.gpsimd
        def _(pool):
            nc.gpsimd.memset(ones[:, :], 1.0).then_inc(ones_done, 1)

            def w_lo_of(i):
                pool.wait_ge(w_hi_done, i + 1)
                nc.gpsimd.tensor_tensor(w_lo[:, w_cols[i]], w_raw[i], w_hi[:, w_cols[i]].bitcast(F32), ALU.subtract
                                        ).then_inc(w_lo_done[i], 1)

            w_lo_of(0)
            pool.wait_ge(bn_chain, 9)

            def x1_and_u(b, slot):
                for s in range(2):
                    n = 2 * b + s
                    at = x_ring[:, slot, s]
                    if not (isinstance(b, int) and n == 1):
                        pool.wait_ge(f1_again, n + 1)
                        pool.wait_ge(m_done, n + 1)
                        nc.gpsimd.tensor_tensor(scratch[:, s], scratch[:, s],
                                                m_all[:, s].unsqueeze(1).to_broadcast([P, CJ, S]),
                                                ALU.mult).then_inc(m_f1, 1)
                    pool.wait_ge(m_f1, n + 1)
                    nc.gpsimd.tensor_tensor(at, scratch[:, s], at, ALU.add).then_inc(x1_done, 1)
                if isinstance(b, int) and b == 0:
                    w_lo_of(1)
                pool.wait_ge(affine_done[1], b + 1)
                after(pool, u_done, 2 * b)
                nc.gpsimd.tensor_tensor(u_scale, affine2[:, 0, :, 0], ones[:, 0:1].to_broadcast([P, 2]), ALU.add)
                nc.gpsimd.tensor_tensor(u_shift, affine2[:, 0, :, 1:2].to_broadcast([P, 2, CJ]),
                                        bn_shift[:, BN_LAST:].unsqueeze(1).to_broadcast([P, 2, CJ]), ALU.add
                                        ).then_inc(u_terms, 1)
                for s in range(2):
                    n = 2 * b + s
                    at = x_ring[:, slot, s]
                    pool.wait_ge(u_terms, b + 1)
                    pool.wait_ge(f2_full, n + 1)
                    pool.wait_ge(pieces_done[1], n + 1)
                    nc.gpsimd.tensor_tensor(u_gate[:, s:s + 1], u_scale[:, s:s + 1], ones[:, :], ALU.mult)
                    for c in range(CJ):
                        last = nc.gpsimd.tensor_scalar(at[:, c], at[:, c], u_scale[:, s:s + 1], u_shift[:, s, c:c + 1],
                                                       ALU.mult, ALU.add)
                    last.then_inc(u_done, 1)

            def step(t, slot, visit):
                if valid(t + 1):
                    x1_and_u(t + 1, slot(1))

            x1_and_u(0, 0)
            steps(pool, step)

        @block.scalar
        def _(act):
            act.wait_ge(bn_loaded, 16)
            act.wait_ge(bn_chain, 1)
            nc.scalar.activation(bn_std[:, :], bn_in[:, 3, :], ACT.Sqrt).then_inc(bn_std_done, 1)

            def w_hi_of(i):
                act.wait_ge(weights_loaded[i], 16)
                nc.scalar.activation(w_hi[:, w_cols[i]], w_raw[i], ACT.Copy).then_inc(w_hi_done, 1)

            def root_var(n, j):
                act.wait_ge(var_done[n], j + 1)
                nc.scalar.activation(std[n][:, :], var[n][:, :], ACT.Sqrt).then_inc(std_done[n], 1)

            def f1_of(j, s, slot):
                act.wait_ge(affine_done[0], j + 1)
                after(act, f2_lo, 2 * j + s - 3)
                nc.scalar.activation(f_full[:, s], x_ring[:, slot, s], ACT.Identity,
                                     bias=affine1[:, slot, s, 1:2], scale=affine1[:, slot, s, 0:1]
                                     ).then_inc(f1_full, 1)

            def f1_again_of(j, s, slot):
                if isinstance(j, int) and j == 0:
                    act.wait_ge(w_lo_done[0], 1)
                after(act, x1_done, 2 * j + s - 1)
                nc.scalar.activation(scratch[:, s], x_ring[:, slot, s], ACT.Identity,
                                     bias=affine1[:, slot, s, 1:2], scale=affine1[:, slot, s, 0:1]
                                     ).then_inc(f1_again, 1)

            def f1_hi_of(j, s):
                act.wait_ge(f1_full, 2 * j + s + 1)
                after(act, gram_done, 2 * j + s)
                nc.scalar.activation(fa[:, :, 0], f_full[:, s], ACT.Copy).then_inc(f1_hi, 1)

            def f2_of(j, s, slot):
                act.wait_ge(affine_done[1], j + 1)
                if valid(j + 1):
                    act.wait_ge(f1_lo, 2 * j + s + 3)
                nc.scalar.activation(f_full[:, s], x_ring[:, slot, s], ACT.Identity,
                                     bias=affine2[:, 0, s, 1:2], scale=affine2[:, 0, s, 0:1]
                                     ).then_inc(f2_full, 1)

            def f2_hi_of(j, s):
                act.wait_ge(f2_full, 2 * j + s + 1)
                after(act, filled[1], 3 * j - 2)
                nc.scalar.activation(fb_hi[:, s], f_full[:, s], ACT.Copy).then_inc(f2_hi, 1)

            def copy_hl(j, s):
                act.wait_ge(diag_chain, 2 * (2 * j + s) + 1)
                nc.scalar.activation(hl0[:, :], gram_ps[s][:, S:2 * S], ACT.Copy)
                nc.scalar.activation(hl1[:, :], corner_ps[0:S1, S1:S1 + S], ACT.Copy).then_inc(hl_copied, 1)

            def root_d(j, s):
                act.wait_ge(clamped, 2 * j + s + 1)
                nc.scalar.activation(d0[:, s], d0[:, s], ACT.Sqrt, bias=sq0[:, s:s + 1], scale=-1.0)
                nc.scalar.activation(d1[:, s], d1[:, s], ACT.Sqrt, bias=sq1[:, s:s + 1], scale=-1.0
                                     ).then_inc(rooted, 1)

            def m_of(j, s):
                act.wait_ge(m_spread, 2 * j + s + 1)
                after(act, m_f1, 2 * j + s - 1)
                nc.scalar.activation(m_all[:, s], gram_ps[s][:, 0:S], ACT.Copy).then_inc(m_done, 1)

            def square(t, layer, m):
                bank = 2 * layer + m
                if layer == 0:
                    act.wait_ge(added[m], 2 * t)
                act.wait_ge(filled[bank], 3 * t + 1)
                if layer == 0:
                    to = z[:, m].rearrange("p (n s) -> p s n", s=2)
                    y = conv_ps[bank][:, 0:2 * S].rearrange("p (s n) -> p s n", s=2)
                else:
                    to, y = z[:, m], conv_ps[bank][:, 0:2 * S]
                nc.scalar.activation(to, y, ACT.Square, bias=1.0).then_inc(squared[bank], 1)

            def h_hi_of(t, layer, m):
                act.wait_ge(h_affine[layer], 2 * t + m + 1)
                nc.scalar.activation(h_parts[layer][0][:, m], z[:, m], ACT.Copy).then_inc(h_hi[layer], 1)

            def square_last(t, j):
                bank, buf = j % BANKS, (j + MC) % ZB
                act.wait_ge(filled[bank], 3 * t + 2 + j // BANKS)
                act.wait_ge(added[buf], 2 * t + j // ZB)
                nc.scalar.activation(z[:, buf].rearrange("p (s n) -> p s n", s=2),
                                     conv_ps[bank][:, 0:2 * S].rearrange("p (n s) -> p s n", s=2),
                                     ACT.Square, bias=1.0).then_inc(squared[bank], 1)

            def step(t, slot, visit):
                a, b, c, e = valid(t + 2), valid(t + 1), valid(t), valid(t + 3)
                if a:
                    f1_of(t + 2, 0, slot(2))
                    f1_hi_of(t + 2, 0)
                if c:
                    square(t, 0, 0)
                if b:
                    m_of(t + 1, 1)
                if c:
                    h_hi_of(t, 0, 0)
                if a:
                    f1_of(t + 2, 1, slot(2))
                if c:
                    square(t, 0, 1)
                    h_hi_of(t, 0, 1)
                if a:
                    f1_hi_of(t + 2, 1)
                    copy_hl(t + 2, 0)
                    f1_again_of(t + 2, 0, slot(2))
                    f1_again_of(t + 2, 1, slot(2))
                    root_d(t + 2, 0)
                if b:
                    root_var(1, t + 1)
                if c:
                    square(t, 1, 0)
                    h_hi_of(t, 1, 0)
                if b:
                    f2_of(t + 1, 0, slot(1))
                    f2_hi_of(t + 1, 0)
                    f2_of(t + 1, 1, slot(1))
                    f2_hi_of(t + 1, 1)
                if c:
                    square(t, 1, 1)
                    h_hi_of(t, 1, 1)
                if a:
                    m_of(t + 2, 0)
                    copy_hl(t + 2, 1)
                if c:
                    for j in range(0, 4):
                        square_last(t, j)
                if a:
                    root_d(t + 2, 1)
                if c:
                    for j in range(4, 7):
                        square_last(t, j)
                if e:
                    root_var(0, t + 3)
                if c:
                    square_last(t, 7)

            root_var(0, 0)
            f1_of(0, 0, 0)
            f1_hi_of(0, 0)
            f1_of(0, 1, 0)
            w_hi_of(0)
            f1_hi_of(0, 1)
            copy_hl(0, 0)
            root_d(0, 0)
            f1_again_of(0, 0, 0)
            f1_again_of(0, 1, 0)
            root_var(0, 1)
            w_hi_of(1)
            m_of(0, 0)
            copy_hl(0, 1)
            f1_of(1, 0, 1)
            root_d(0, 1)
            f1_hi_of(1, 0)
            f1_of(1, 1, 1)
            m_of(0, 1)
            w_hi_of(2)
            f1_hi_of(1, 1)
            copy_hl(1, 0)
            root_var(1, 0)
            f2_of(0, 0, 0)
            f2_hi_of(0, 0)
            root_d(1, 0)
            f2_of(0, 1, 0)
            f2_hi_of(0, 1)
            copy_hl(1, 1)
            f1_again_of(1, 0, 1)
            f1_again_of(1, 1, 1)
            m_of(1, 0)
            root_var(0, 2)
            root_d(1, 1)
            steps(act, step)

        @block.vector
        def _(dve):
            dve.wait_ge(bn_loaded, 16)
            nc.vector.tensor_scalar_add(bn_in[:, 3, :], bn_in[:, 3, :], BN_EPS).then_inc(bn_chain, 1)
            dve.wait_ge(eye_loaded, 16)
            nc.vector.tensor_copy(eye, eye_raw)
            nc.vector.tensor_scalar(eye_once_twice[:, 1], eye_raw, 2.0, None, ALU.mult).then_inc(eye_done, 1)
            dve.wait_ge(const_loaded, 16)

            def batchnorm():
                dve.wait_ge(bn_std_done, 1)
                nc.vector.reciprocal(bn_std[:, :], bn_std[:, :]).then_inc(bn_chain, 1)
                dve.wait_ge(bn_chain, 2)
                nc.vector.tensor_tensor(bn_scale[:, :], bn_in[:, 3, :], bn_std[:, :], ALU.mult).then_inc(bn_chain, 1)
                dve.wait_ge(bn_chain, 3)
                nc.vector.tensor_tensor(bn_scale[:, :], bn_scale[:, :], bn_std[:, :], ALU.mult).then_inc(bn_chain, 1)
                dve.wait_ge(bn_chain, 4)
                nc.vector.tensor_scalar(bn_scale[:, :], bn_scale[:, :], -0.5, 1.5, ALU.mult, ALU.add
                                        ).then_inc(bn_chain, 1)
                dve.wait_ge(bn_chain, 5)
                nc.vector.tensor_tensor(bn_std[:, :], bn_scale[:, :], bn_std[:, :], ALU.mult).then_inc(bn_chain, 1)
                dve.wait_ge(bn_chain, 6)
                nc.vector.tensor_tensor(bn_scale[:, :], bn_in[:, 0, :], bn_std[:, :], ALU.mult).then_inc(bn_chain, 1)
                dve.wait_ge(bn_chain, 7)
                nc.vector.tensor_tensor(bn_shift[:, :], bn_in[:, 2, :], bn_scale[:, :], ALU.mult).then_inc(bn_chain, 1)
                dve.wait_ge(bn_chain, 8)
                nc.vector.tensor_tensor(bn_shift[:, :], bn_in[:, 1, :], bn_shift[:, :], ALU.subtract).then_inc(bn_chain, 1)

            def stat_pieces(n, j, s, slot):
                row = x_ring[:, slot, s].rearrange("p (a j) n -> p a (j n)", a=STAT_PIECES)
                for a in range(STAT_PIECES):
                    last = nc.vector.bn_stats(pieces[n][:, s, a, :], row[:, a])
                last.then_inc(pieces_done[n], 1)

            def moments_of(n, j):
                dve.wait_ge(pieces_done[n], 2 * j + 2)
                nc.vector.tensor_copy(mean_sq[n][:, 0:1], pieces[n][:, 1, 0, 0:1])
                for s in range(2):
                    last = nc.vector.bn_aggr(moments[n][:, s, :], pieces[n][:, s].rearrange("p a e -> p (a e)"))
                last.then_inc(moments_chain[n], 1)
                dve.wait_ge(moments_chain[n], 2 * j + 1)
                nc.vector.tensor_tensor(mean_sq[n][:, :], moments[n][:, :, 0], moments[n][:, :, 0], ALU.mult
                                        ).then_inc(moments_chain[n], 1)
                dve.wait_ge(moments_chain[n], 2 * j + 2)
                nc.vector.tensor_tensor(moments[n][:, :, 1], moments[n][:, :, 1], mean_sq[n][:, :], ALU.add
                                        ).then_inc(moments_done[n], 1)

            def group_var(n, j):
                dve.wait_ge(group_summed[n], j + 1)
                nc.vector.tensor_copy(group[n][:, :, :].rearrange("p s e -> p (s e)"), stat_ps[:, 4 * n:4 * n + 4]
                                      ).then_inc(var_chain[n], 1)
                dve.wait_ge(var_chain[n], 3 * j + 1)
                nc.vector.tensor_tensor(mean_sq[n][:, :], group[n][:, :, 0], group[n][:, :, 0], ALU.mult
                                        ).then_inc(var_chain[n], 1)
                dve.wait_ge(var_chain[n], 3 * j + 2)
                nc.vector.tensor_tensor(var[n][:, :], group[n][:, :, 1], mean_sq[n][:, :], ALU.subtract
                                        ).then_inc(var_chain[n], 1)
                dve.wait_ge(var_chain[n], 3 * j + 3)
                nc.vector.tensor_scalar(var[n][:, :], var[n][:, :], 0.0, GN_EPS, ALU.max, ALU.add
                                        ).then_inc(var_done[n], 1)

            def affine_of(n, j, to):
                dve.wait_ge(std_done[n], j + 1)
                nc.vector.reciprocal(rec[n][:, :], std[n][:, :]).then_inc(scale_chain[n], 1)
                dve.wait_ge(scale_chain[n], 5 * j + 1)
                nc.vector.tensor_tensor(mean_sq[n][:, :], var[n][:, :], rec[n][:, :], ALU.mult
                                        ).then_inc(scale_chain[n], 1)
                dve.wait_ge(scale_chain[n], 5 * j + 2)
                nc.vector.tensor_tensor(mean_sq[n][:, :], mean_sq[n][:, :], rec[n][:, :], ALU.mult
                                        ).then_inc(scale_chain[n], 1)
                dve.wait_ge(scale_chain[n], 5 * j + 3)
                nc.vector.tensor_scalar(mean_sq[n][:, :], mean_sq[n][:, :], -0.5, 1.5, ALU.mult, ALU.add
                                        ).then_inc(scale_chain[n], 1)
                dve.wait_ge(scale_chain[n], 5 * j + 4)
                nc.vector.tensor_tensor(to[:, :, 0], mean_sq[n][:, :], rec[n][:, :], ALU.mult
                                        ).then_inc(scale_chain[n], 1)
                dve.wait_ge(scale_chain[n], 5 * j + 5)
                nc.vector.scalar_tensor_tensor(to[:, :, 1], group[n][:, :, 0], -1.0, to[:, :, 0],
                                               ALU.mult, ALU.mult).then_inc(affine_done[n], 1)

            def w_lo_last():
                dve.wait_ge(w_hi_done, 3)
                nc.vector.tensor_tensor(w_lo[:, w_cols[2]], w_raw[2], w_hi[:, w_cols[2]].bitcast(F32), ALU.subtract
                                        ).then_inc(w_lo_done[2], 1)

            def f1_lo_of(j, s):
                dve.wait_ge(f1_hi, 2 * j + s + 1)
                nc.vector.tensor_tensor(fa[:, :, 1], f_full[:, s], fa[:, :, 0].bitcast(F32), ALU.subtract
                                        ).then_inc(f1_lo, 1)

            def f2_lo_of(j, s):
                dve.wait_ge(f2_hi, 2 * j + s + 1)
                nc.vector.tensor_tensor(fb_lo[:, s], f_full[:, s], fb_hi[:, s].bitcast(F32), ALU.subtract
                                        ).then_inc(f2_lo, 1)

            def diag_of(j, s):
                n = 2 * j + s
                dve.wait_ge(gram_done, n + 1)
                nc.vector.tensor_tensor_reduce(
                    out=d0[:, :, 0:P], in0=gram_ps[s][:, 0:2 * S].rearrange("p (a n) -> p a n", a=2)[:, :, 0:P],
                    in1=eye_once_twice[:, :, :].bitcast(F32),
                    scale=1.0, scalar=0.0, op0=ALU.mult, op1=ALU.add, accum_out=sq0[:, s:s + 1])
                nc.vector.tensor_tensor_reduce(
                    out=d1[:, :, :], in0=corner_ps[0:S1, 0:2 * S].rearrange("p (a n) -> p a n", a=2)[:, :, 0:S1],
                    in1=eye_once_twice[0:S1, :, 0:S1].bitcast(F32),
                    scale=1.0, scalar=0.0, op0=ALU.mult, op1=ALU.add, accum_out=sq1[:, s:s + 1]
                    ).then_inc(diag_chain, 1)
                dve.wait_ge(diag_chain, 2 * n + 1)
                nc.vector.tensor_scalar(pixel0[:, s, 0:1], sq0[:, s:s + 1], -0.5, None, ALU.mult)
                nc.vector.tensor_scalar(pixel1[:, s, 0:1], sq1[:, s:s + 1], -0.5, None, ALU.mult
                                        ).then_inc(diag_chain, 1)
                dve.wait_ge(diag_chain, 2 * n + 2)
                nc.vector.scalar_tensor_tensor(pixel0[:, s, 1:2], sq0[:, s:s + 1], -0.5,
                                               pixel0[:, s, 0:1].bitcast(F32), ALU.mult, ALU.subtract)
                nc.vector.scalar_tensor_tensor(pixel1[:, s, 1:2], sq1[:, s:s + 1], -0.5,
                                               pixel1[:, s, 0:1].bitcast(F32), ALU.mult, ALU.subtract
                                               ).then_inc(diag_done, 1)

            def clamp(j, s):
                n = 2 * j + s
                dve.wait_ge(hl_copied, n + 1)
                dve.wait_ge(rows_added, n + 1)
                nc.vector.tensor_tensor(d0[:, s], gram_ps[s][:, 0:S], hl0[:, :].bitcast(F32), ALU.add)
                nc.vector.tensor_tensor(d1[:, s], corner_ps[0:S1, 0:S1], hl1[:, P:S].bitcast(F32), ALU.add
                                        ).then_inc(clamp_chain, 1)
                dve.wait_ge(clamp_chain, n + 1)
                nc.vector.tensor_scalar(d0[:, s], d0[:, s], 2.0, sq0[:, s:s + 1], ALU.mult, ALU.min)
                nc.vector.tensor_scalar(d1[:, s], d1[:, s], 2.0, sq1[:, s:s + 1], ALU.mult, ALU.min
                                        ).then_inc(clamped, 1)

            def damp(j, s):
                dve.wait_ge(rooted, 2 * j + s + 1)
                nc.vector.tensor_tensor_reduce(out=d0[:, s], in0=d0[:, s], in1=dist0, scale=1.0, scalar=0.0,
                                               op0=ALU.mult, op1=ALU.add, accum_out=sum0[:, s:s + 1])
                nc.vector.tensor_tensor(d1[:, s], d1[:, s], dist1, ALU.mult).then_inc(damped, 1)

            def new_m(j, s):
                n = 2 * j + s
                dve.wait_ge(sums_done, n + 1)
                nc.vector.tensor_copy(sum1[:, s:s + 1], gram_ps[s][0:S1, S:S + 1])
                nc.vector.reciprocal(rec0[:, s:s + 1], sum0[:, s:s + 1]).then_inc(m_chain, 1)
                dve.wait_ge(m_chain, 3 * n + 1)
                nc.vector.reciprocal(rec1[:, s:s + 1], sum1[:, s:s + 1]).then_inc(m_chain, 1)
                dve.wait_ge(m_chain, 3 * n + 2)
                for to in (m0[:, s:s + 1], pixel0[:, s, 0:1]):
                    nc.vector.tensor_scalar(to, sum0[:, s:s + 1], 1.0 / S, rec0[:, s:s + 1], ALU.mult, ALU.mult)
                for to in (m1[:, s:s + 1], pixel1[:, s, 0:1]):
                    last = nc.vector.tensor_scalar(to, sum1[:, s:s + 1], 1.0 / S, rec1[:, s:s + 1],
                                                   ALU.mult, ALU.mult)
                last.then_inc(m_chain, 1)
                dve.wait_ge(m_chain, 3 * n + 3)
                nc.vector.tensor_tensor(pixel0[:, s, 1:2], m0[:, s:s + 1], pixel0[:, s, 0:1].bitcast(F32),
                                        ALU.subtract)
                nc.vector.tensor_tensor(pixel1[:, s, 1:2], m1[:, s:s + 1], pixel1[:, s, 0:1].bitcast(F32),
                                        ALU.subtract).then_inc(m_split, 1)

            def h_affine_of(t, layer, m):
                col = MC * layer + m
                dve.wait_ge(squared[2 * layer + m], 3 * t + 1)
                nc.vector.tensor_scalar(z[:, m], z[:, m], bn_scale[:, col:col + 1], bn_shift[:, col:col + 1],
                                        ALU.mult, ALU.add).then_inc(h_affine[layer], 1)

            def h_lo_of(t, layer, m):
                dve.wait_ge(h_hi[layer], 2 * t + m + 1)
                hi, lo = h_parts[layer]
                nc.vector.tensor_tensor(lo[:, m], z[:, m], hi[:, m].bitcast(F32), ALU.subtract).then_inc(h_lo[layer], 1)

            def add_last(t, j, slot):
                if j == 0:
                    dve.wait_ge(u_done, 2 * t + 2)
                dve.wait_ge(squared[j % BANKS], 3 * t + 2 + j // BANKS)
                at, buf = x_ring[:, slot, :, j], (j + MC) % ZB
                nc.vector.scalar_tensor_tensor(at, z[:, buf].rearrange("p (s n) -> p s n", s=2),
                                               bn_scale[:, BN_LAST + j:BN_LAST + j + 1], at,
                                               ALU.mult, ALU.add).then_inc(added[buf], 1)

            def step(t, slot, visit):
                a, b, c, e = valid(t + 2), valid(t + 1), valid(t), valid(t + 3)
                if b:
                    new_m(t + 1, 1)
                if a:
                    f1_lo_of(t + 2, 0)
                if c:
                    h_affine_of(t, 0, 0)
                    h_lo_of(t, 0, 0)
                if b:
                    dve.wait_ge(x1_done, 2 * (t + 1) + 1)
                    stat_pieces(1, t + 1, 0, slot(1))
                if c:
                    h_affine_of(t, 0, 1)
                    h_lo_of(t, 0, 1)
                if a:
                    diag_of(t + 2, 0)
                if b:
                    dve.wait_ge(x1_done, 2 * (t + 1) + 2)
                    stat_pieces(1, t + 1, 1, slot(1))
                    moments_of(1, t + 1)
                if a:
                    f1_lo_of(t + 2, 1)
                    clamp(t + 2, 0)
                if b:
                    group_var(1, t + 1)
                    affine_of(1, t + 1, affine2[:, 0])
                if c:
                    h_affine_of(t, 1, 0)
                if a:
                    damp(t + 2, 0)
                if e:
                    dve.wait_ge(x_loaded[slot(3)], 32 * visit(3) + 32)
                    stat_pieces(0, t + 3, 0, slot(3))
                if c:
                    h_lo_of(t, 1, 0)
                if a:
                    new_m(t + 2, 0)
                if b:
                    f2_lo_of(t + 1, 0)
                if e:
                    stat_pieces(0, t + 3, 1, slot(3))
                    moments_of(0, t + 3)
                if c:
                    h_affine_of(t, 1, 1)
                    h_lo_of(t, 1, 1)
                if a:
                    diag_of(t + 2, 1)
                if c:
                    add_last(t, 0, slot(0))
                if c:
                    add_last(t, 1, slot(0))
                if a:
                    clamp(t + 2, 1)
                if c:
                    add_last(t, 2, slot(0))
                if b:
                    f2_lo_of(t + 1, 1)
                if c:
                    add_last(t, 3, slot(0))
                if a:
                    damp(t + 2, 1)
                if c:
                    add_last(t, 4, slot(0))
                if e:
                    group_var(0, t + 3)
                if c:
                    add_last(t, 5, slot(0))
                if c:
                    add_last(t, 6, slot(0))
                if c:
                    add_last(t, 7, slot(0))
                if e:
                    affine_of(0, t + 3, affine1[:, slot(3)])

            dve.wait_ge(x_loaded[0], 32)
            for s in range(2):
                stat_pieces(0, 0, s, 0)
            moments_of(0, 0)
            group_var(0, 0)
            affine_of(0, 0, affine1[:, 0])
            batchnorm()
            f1_lo_of(0, 0)
            dve.wait_ge(x_loaded[1], 32)
            for s in range(2):
                stat_pieces(0, 1, s, 1)
            moments_of(0, 1)
            diag_of(0, 0)
            clamp(0, 0)
            f1_lo_of(0, 1)
            damp(0, 0)
            new_m(0, 0)
            group_var(0, 1)
            affine_of(0, 1, affine1[:, 1])
            diag_of(0, 1)
            clamp(0, 1)
            damp(0, 1)
            new_m(0, 1)
            dve.wait_ge(m_f1, 1)
            dve.wait_ge(f1_again, 2)
            dve.wait_ge(m_done, 2)
            nc.vector.tensor_tensor(scratch[:, 1], scratch[:, 1], m_all[:, 1].unsqueeze(1).to_broadcast([P, CJ, S]),
                                    ALU.mult).then_inc(m_f1, 1)
            f1_lo_of(1, 0)
            dve.wait_ge(x1_done, 1)
            stat_pieces(1, 0, 0, 0)
            dve.wait_ge(x1_done, 2)
            stat_pieces(1, 0, 1, 0)
            moments_of(1, 0)
            diag_of(1, 0)
            group_var(1, 0)
            affine_of(1, 0, affine2[:, 0])
            f1_lo_of(1, 1)
            clamp(1, 0)
            f2_lo_of(0, 0)
            damp(1, 0)
            f2_lo_of(0, 1)
            dve.wait_ge(sums_done, 3)
            diag_of(1, 1)
            w_lo_last()
            new_m(1, 0)
            dve.wait_ge(x_loaded[2], 32)
            for s in range(2):
                stat_pieces(0, 2, s, 2)
            moments_of(0, 2)
            group_var(0, 2)
            clamp(1, 1)
            affine_of(0, 2, affine1[:, 2])
            damp(1, 1)
            steps(dve, step)

        @block.tensor
        def _(pe):
            pe.wait_ge(ones_done, 1)
            pe.wait_ge(const_loaded, 16)
            pe.wait_ge(eye_done, 1)

            def gram(j, s):
                n = 2 * j + s
                after(pe, m_done, n - 1)
                pe.wait_ge(f1_lo, n + 1)
                for c in range(CJ):
                    nc.tensor.matmul(gram_ps[s][:, 0:2 * S], fa[:, c, 0, 0:P],
                                     fa[:, c].rearrange("p a n -> p (a n)"),
                                     start=c == 0, stop=False, skip_group_check=True)
                after(pe, clamped, n)
                for c in range(CJ):
                    last = nc.tensor.matmul(corner_ps[0:S1, 0:S1 + S], fa[:, c, 0, P:S],
                                            fa[:, c].rearrange("p a n -> p (a n)")[:, P:2 * S],
                                            start=c == 0, stop=False, skip_group_check=True)
                last.then_inc(gram_done, 1)

            def add_lh(s):
                nc.tensor.matmul(gram_ps[s][:, 0:P], hl0[:, 0:P], eye, start=False, stop=False,
                                 skip_group_check=True)
                nc.tensor.matmul(gram_ps[s][:, P:S], hl1[:, 0:P], eye[0:S1, 0:S1], start=False, stop=False,
                                 skip_group_check=True)
                nc.tensor.matmul(corner_ps[0:S1, 0:S1], hl1[:, P:S], eye[0:S1, 0:S1], start=False, stop=False,
                                 skip_group_check=True)

            def spread_pixels(s, other_rows, start):
                for i in range(2):
                    of0 = pixel0[:, s, i:i + 1].to_broadcast([P, P])
                    of1 = pixel1[:, s, i:i + 1].to_broadcast([S1, P])
                    nc.tensor.matmul(gram_ps[s][:, 0:P], of0, eye, start=start and i == 0, stop=False,
                                     skip_group_check=True)
                    last = nc.tensor.matmul(gram_ps[s][:, P:S], of1, eye[0:S1, 0:S1], start=False, stop=i == 1,
                                            skip_group_check=True)
                    if other_rows:
                        last = nc.tensor.matmul(corner_ps[0:S1, 0:S1], pixel1[:, s, i:i + 1].to_broadcast([S1, S1]),
                                                eye[0:S1, 0:S1], start=False, stop=i == 1, skip_group_check=True)
                return last

            def add_rows(j, s):
                pe.wait_ge(diag_done, 2 * j + s + 1)
                pe.wait_ge(hl_copied, 2 * j + s + 1)
                add_lh(s)
                spread_pixels(s, other_rows=True, start=False).then_inc(rows_added, 1)

            def sum_rows(j, s):
                pe.wait_ge(damped, 2 * j + s + 1)
                nc.tensor.matmul(gram_ps[s][0:S1, S:S + 1], d0[:, s, P:S], ones[:, :], start=True, stop=False)
                nc.tensor.matmul(gram_ps[s][0:S1, S:S + 1], d1[:, s], ones[0:S1, :], start=False, stop=True
                                 ).then_inc(sums_done, 1)

            def spread_m(j, s):
                pe.wait_ge(m_split, 2 * j + s + 1)
                spread_pixels(s, other_rows=False, start=True).then_inc(m_spread, 1)

            def sum_group(n, j):
                pe.wait_ge(moments_done[n], j + 1)
                if n == 1 and valid(j + 1):
                    after(pe, var_chain[0], 3 * j + 4)
                if n == 0:
                    after(pe, var_chain[1], 3 * j - 5)
                nc.tensor.matmul(stat_ps[:, 4 * n:4 * n + 4], group_mean,
                                 moments[n][:, :, :].rearrange("p s e -> p (s e)"),
                                 start=True, stop=True).then_inc(group_summed[n], 1)

            def conv1(t, m):
                if isinstance(t, int) and t == 0 and m == 0:
                    pe.wait_ge(w_lo_done[0], 1)
                if m == 0:
                    pe.wait_ge(f2_lo, 2 * t + 2)
                pe.wait_ge(squared[m], 3 * t)
                for j in range(CJ):
                    for i, (w, f) in enumerate(PRODUCTS):
                        last = nc.tensor.matmul(conv_ps[m][:, 0:2 * S], w1[w][:, j, m * P:(m + 1) * P],
                                                fb[f][:, :, j], start=(j == 0 and i == 0),
                                                stop=(j == CJ - 1 and i == 2))
                last.then_inc(filled[m], 1)

            def conv2(t, m, k, taps=(1, 0, 2)):
                bank = 2 + m
                if isinstance(t, int) and t == 0 and m == 0 and k == 0:
                    pe.wait_ge(w_lo_done[1], 1)
                    pe.wait_ge(w_lo_done[2], 1)
                if k == 0:
                    pe.wait_ge(squared[bank], 3 * t)
                if m == 0 and 1 in taps:
                    pe.wait_ge(h_lo[0], 2 * t + k + 1)
                for dy in taps:
                    top, bottom = max(1 - dy, 0), SIDE - max(dy - 1, 0)
                    for dx in (1, 0, 2):
                        left, right = max(1 - dx, 0), SIDE - max(dx - 1, 0)
                        to = conv_ps[bank][:, 0:2 * S].rearrange("p (h w) -> p h w", h=SIDE)[
                            :, top:bottom, 2 * left:2 * right]
                        for i, (w, f) in enumerate(PRODUCTS):
                            last = nc.tensor.matmul(to, w2[w][:, k, 3 * dy + dx, m * P:(m + 1) * P],
                                                    h1[f][:, k, top + dy - 1:bottom + dy - 1,
                                                          2 * (left + dx - 1):2 * (right + dx - 1)],
                                                    start=(k == 0 and dy == 1 and dx == 1 and i == 0),
                                                    stop=(k == MC - 1 and dy == 2 and dx == 2 and i == 2))
                if k == MC - 1 and 2 in taps:
                    last.then_inc(filled[bank], 1)

            def conv3(t, j, inputs=range(MC)):
                bank = j % BANKS
                if 0 in inputs:
                    pe.wait_ge(squared[bank], 3 * t + 1 + j // BANKS)
                for k in inputs:
                    if j == 0:
                        pe.wait_ge(h_lo[1], 2 * t + k + 1)
                    for i, (w, f) in enumerate(PRODUCTS):
                        last = nc.tensor.matmul(conv_ps[bank][:, 0:2 * S], w3[w][k][:, j], h2[f][:, k],
                                                start=(k == 0 and i == 0), stop=(k == MC - 1 and i == 2))
                if MC - 1 in inputs:
                    last.then_inc(filled[bank], 1)

            def step(t):
                a, b, c, e = valid(t + 2), valid(t + 1), valid(t), valid(t + 3)
                if c:
                    conv1(t, 0)
                if isinstance(t, int) and t == 0:
                    conv1(0, 1)
                    spread_m(1, 0)
                    sum_group(0, 2)
                    add_rows(1, 1)
                    sum_rows(1, 1)
                    spread_m(1, 1)
                else:
                    if b:
                        spread_m(t + 1, 1)
                    if c:
                        conv1(t, 1)
                if a:
                    gram(t + 2, 0)
                if c:
                    conv2(t, 0, 0)
                if a:
                    add_rows(t + 2, 0)
                if c:
                    conv2(t, 0, 1, taps=[1])
                if b:
                    sum_group(1, t + 1)
                if c:
                    conv2(t, 0, 1, taps=[0, 2])
                    conv2(t, 1, 0)
                if a:
                    sum_rows(t + 2, 0)
                if c:
                    conv2(t, 1, 1)
                if a:
                    spread_m(t + 2, 0)
                    gram(t + 2, 1)
                if c:
                    for k in range(MC):
                        for j in range(0, 2):
                            conv3(t, j, inputs=[k])
                if a:
                    add_rows(t + 2, 1)
                if c:
                    for j in range(2, 6):
                        conv3(t, j)
                if e:
                    sum_group(0, t + 3)
                if c:
                    for j in range(6, 8):
                        conv3(t, j)
                if a:
                    sum_rows(t + 2, 1)

            sum_group(0, 0)
            gram(0, 0)
            sum_group(0, 1)
            add_rows(0, 0)
            sum_rows(0, 0)
            gram(0, 1)
            spread_m(0, 0)
            add_rows(0, 1)
            sum_rows(0, 1)
            spread_m(0, 1)
            gram(1, 0)
            sum_group(1, 0)
            add_rows(1, 0)
            gram(1, 1)
            sum_rows(1, 0)
            step(0)
            if pairs > 4:
                with pe.Fori(1, pairs - 3) as t:
                    step(t)
            for t in range(max(pairs - 3, 0), pairs):
                step(t)


def constants():
    import numpy as np

    at = np.stack(np.meshgrid(np.arange(SIDE), np.arange(SIDE), indexing="ij")).reshape(2, -1)
    d2 = ((at[:, :, None] - at[:, None, :]) ** 2).sum(0).astype(np.float32)
    dist = np.exp(-d2 / np.float32(2.0 * (0.15 * SIDE) ** 2)).astype(np.float32)
    table = np.zeros((P, CONSTS), np.float32)
    table[:, 0:S] = dist[0:P]
    table[0:S1, S:S + S1] = dist[P:, P:]
    p = np.arange(P) // GROUP_PARTS
    table[:, S + S1:] = (p[:, None] == p[None, :]) / np.float32(GROUP_PARTS)
    return table


def laid_out(inputs):
    import numpy as np

    a = {k: np.asarray(v) for k, v in inputs.items()}
    w1 = a["L1_conv_w1"].reshape(MID, P, CJ).transpose(1, 2, 0).reshape(P, W1)
    w2 = a["L1_conv_w2"].reshape(MID, MC, P, TAPS).transpose(2, 1, 3, 0).reshape(P, W2)
    w3 = a["L1_conv_w3"].reshape(P, CJ, MC, P).transpose(3, 2, 1, 0).reshape(P, MC, C)
    bn = []
    for what in "gbmv":
        cols = [a[f"L1_conv_{what}{i}"].reshape(MC, P).T for i in (1, 2)]
        bn.append(np.concatenate(cols + [a[f"L1_conv_{what}3"].reshape(P, CJ)], axis=1))
    return {
        "x": np.ascontiguousarray(a["x"]),
        "weights": np.ascontiguousarray(np.concatenate([w1, w3[:, 0], w2, w3[:, 1]], axis=1)),
        "bn": np.ascontiguousarray(np.stack(bn, axis=1)),
        "identity": np.eye(P, dtype=np.float32),
        "consts": constants(),
    }


def kernel(**inputs):
    import concourse.bacc as bacc
    from concourse.bass_utils import run_bass_kernel_spmd

    nc = bacc.Bacc("TRN2", target_bir_lowering=False, num_devices=1)
    arrays = laid_out(inputs)
    args = [nc.dram_tensor(n, v.shape, F32, kind="ExternalInput").ap() for n, v in arrays.items()]
    out = nc.dram_tensor("out", arrays["x"].shape, F32, kind="ExternalOutput").ap()
    build(nc, *args, out)
    r = run_bass_kernel_spmd(nc, [arrays], core_ids=[0])
    return r.results[0]["out"]
```
